# Optimizing a Trainium2 kernel written in Bass

```python
import numpy as np
import jax
import jax.numpy as jnp

def _softmax(x, axis=-1):
    return jax.nn.softmax(x, axis=axis)

def _gelu(x):
    return jax.nn.gelu(x, approximate=True)

def _silu(x):
    return jax.nn.silu(x)

def _sigmoid(x):
    return jax.nn.sigmoid(x)

def _layernorm(x, axis=-1, eps=1e-05):
    m = jnp.mean(x, axis=axis, keepdims=True)
    v = jnp.var(x, axis=axis, keepdims=True)
    return (x - m) / jnp.sqrt(v + eps)

def _scatter_add(tgt, idx, src, axis=0):
    return tgt.at[idx].add(src)

def _segment_sum(src, seg, n):
    return jax.ops.segment_sum(src, seg, n)
kernel_name = 'mk_macaron_d1_jaxref_r4_af0282'

def setup_inputs(seed: int=0):
    np.random.seed(seed)
    _w = jnp.asarray

    def _L0_attn_setup():
        import jax, jax.numpy as jnp
        import numpy as np
        NUM_HEADS = 16
        LN_EPS = 1e-05

        def _rope(x):
            S, D = (x.shape[-2], x.shape[-1])
            rot = D // 2
            inv_freq = 1.0 / 10000.0 ** (jnp.arange(0, rot, 2, dtype=jnp.float32) / rot)
            ang = jnp.arange(S, dtype=jnp.float32)[:, None] * inv_freq[None, :]
            ang = jnp.repeat(ang, 2, axis=-1)
            cos, sin = (jnp.cos(ang), jnp.sin(ang))
            xr, xp = (x[..., :rot], x[..., rot:])
            x1, x2 = (xr[..., 0::2], xr[..., 1::2])
            rot_half = jnp.stack((-x2, x1), axis=-1).reshape(xr.shape)
            xr = xr * cos + rot_half * sin
            return jnp.concatenate([xr, xp], axis=-1)
        key = jax.random.key(seed)
        k1, k2, k3 = jax.random.split(key, 3)
        B, S, D = (4, 512, 512)
        X = jax.random.normal(k1, (B, S, D), dtype=jnp.float32)
        ln_w = jnp.ones((D,), dtype=jnp.float32)
        ln_b = jnp.zeros((D,), dtype=jnp.float32)
        W_in = jax.random.normal(k2, (D, 3 * D), dtype=jnp.float32) * 0.02
        W_out = jax.random.normal(k3, (D, D), dtype=jnp.float32) * 0.02
        return {'X': X, 'ln_w': ln_w, 'ln_b': ln_b, 'W_in': W_in, 'W_out': W_out}
    _L0_attn_in = _L0_attn_setup()

    def _L0_ffn_setup():
        import jax, jax.numpy as jnp
        import numpy as np
        E, K, H, F = (64, 6, 512, 192)
        G, KG = (8, 4)
        SHARED_F = 192
        SCALE = 2.5
        T = 2 * 256
        CAP = 2 * (T * K // E)

        def _grouped_topk(logits, bias):
            scores = jax.nn.sigmoid(logits.astype(jnp.float32))
            scores_b = scores + bias[None, :]
            gs = scores_b.reshape(-1, G, E // G)
            group_scores = jnp.sum(jax.lax.top_k(gs, 2)[0], axis=-1)
            gidx = jax.lax.top_k(group_scores, KG)[1]
            rows = jnp.arange(group_scores.shape[0])[:, None]
            group_mask = jnp.zeros_like(group_scores).at[rows, gidx].set(1.0)
            score_mask = jnp.repeat(group_mask, E // G, axis=-1) > 0
            tmp = jnp.where(score_mask, scores_b, -jnp.inf)
            topk_ids = jax.lax.top_k(tmp, K)[1]
            topk_w = jnp.take_along_axis(scores, topk_ids, axis=-1)
            topk_w = topk_w / jnp.sum(topk_w, axis=-1, keepdims=True)
            return (topk_w * SCALE, topk_ids)

        def _routed_moe(x, topk_w, topk_ids, w_gate, w_up, w_down):
            Tn = x.shape[0]
            flat_e = topk_ids.reshape(-1)
            order = jnp.argsort(flat_e)
            se = flat_e[order]
            pos = jnp.arange(Tn * K) - jnp.searchsorted(se, se, side='left')
            tok = order // K
            valid = pos < CAP
            slot = jnp.where(valid, pos, CAP)
            buf = jnp.zeros((E, CAP + 1, H), x.dtype).at[se, slot].set(x[tok])[:, :CAP]
            h = jax.nn.silu(jnp.einsum('ech,ehf->ecf', buf, w_gate)) * jnp.einsum('ech,ehf->ecf', buf, w_up)
            out = jnp.einsum('ecf,efh->ech', h, w_down)
            gathered = out[se, jnp.minimum(pos, CAP - 1)] * valid.astype(x.dtype)[:, None]
            w = topk_w.reshape(-1)[order].astype(x.dtype)[:, None]
            return jax.ops.segment_sum(gathered * w, tok, num_segments=Tn)
        key = jax.random.key(seed)
        ks = jax.random.split(key, 9)
        s = 0.02
        return dict(hidden_states=jax.random.normal(ks[0], (2, 256, H), jnp.float32), gate_w=jax.random.normal(ks[1], (H, E), jnp.float32) * s, bias=jax.random.normal(ks[2], (E,), jnp.float32) * s, w_gate=jax.random.normal(ks[3], (E, H, F), jnp.float32) * s, w_up=jax.random.normal(ks[4], (E, H, F), jnp.float32) * s, w_down=jax.random.normal(ks[5], (E, F, H), jnp.float32) * s, ws_gate=jax.random.normal(ks[6], (H, SHARED_F), jnp.float32) * s, ws_up=jax.random.normal(ks[7], (H, SHARED_F), jnp.float32) * s, ws_down=jax.random.normal(ks[8], (SHARED_F, H), jnp.float32) * s)
    _L0_ffn_in = _L0_ffn_setup()
    _d = {'L0_attn_X': _L0_attn_in['X'], 'L0_attn_ln_w': _L0_attn_in['ln_w'], 'L0_attn_ln_b': _L0_attn_in['ln_b'], 'L0_attn_W_in': _L0_attn_in['W_in'], 'L0_attn_W_out': _L0_attn_in['W_out'], 'L0_ffn_gate_w': _L0_ffn_in['gate_w'], 'L0_ffn_bias': _L0_ffn_in['bias'], 'L0_ffn_w_gate': _L0_ffn_in['w_gate'], 'L0_ffn_w_up': _L0_ffn_in['w_up'], 'L0_ffn_w_down': _L0_ffn_in['w_down'], 'L0_ffn_ws_gate': _L0_ffn_in['ws_gate'], 'L0_ffn_ws_up': _L0_ffn_in['ws_up'], 'L0_ffn_ws_down': _L0_ffn_in['ws_down']}
    _x0 = _d['L0_attn_X']
    _d['L0_attn_X'] = jax.random.normal(jax.random.fold_in(jax.random.key(seed), 1), (4, 512, 512), dtype=_x0.dtype)
    del _x0
    return _d

def reference(L0_attn_X, L0_attn_ln_w, L0_attn_ln_b, L0_attn_W_in, L0_attn_W_out, L0_ffn_gate_w, L0_ffn_bias, L0_ffn_w_gate, L0_ffn_w_up, L0_ffn_w_down, L0_ffn_ws_gate, L0_ffn_ws_up, L0_ffn_ws_down):

    def _L0_attn_ref(X, ln_w, ln_b, W_in, W_out):
        import jax, jax.numpy as jnp
        import numpy as np
        NUM_HEADS = 16
        LN_EPS = 1e-05

        def _rope(x):
            S, D = (x.shape[-2], x.shape[-1])
            rot = D // 2
            inv_freq = 1.0 / 10000.0 ** (jnp.arange(0, rot, 2, dtype=jnp.float32) / rot)
            ang = jnp.arange(S, dtype=jnp.float32)[:, None] * inv_freq[None, :]
            ang = jnp.repeat(ang, 2, axis=-1)
            cos, sin = (jnp.cos(ang), jnp.sin(ang))
            xr, xp = (x[..., :rot], x[..., rot:])
            x1, x2 = (xr[..., 0::2], xr[..., 1::2])
            rot_half = jnp.stack((-x2, x1), axis=-1).reshape(xr.shape)
            xr = xr * cos + rot_half * sin
            return jnp.concatenate([xr, xp], axis=-1)
        B, S, D = X.shape
        H = NUM_HEADS
        Dh = D // H
        mu = jnp.mean(X, axis=-1, keepdims=True)
        var = jnp.mean(jnp.square(X - mu), axis=-1, keepdims=True)
        Xn = (X - mu) * jax.lax.rsqrt(var + LN_EPS) * ln_w + ln_b
        qkv = jnp.einsum('bsd,df->bsf', Xn, W_in)
        Q, K, V = jnp.split(qkv, 3, axis=-1)
        Q = Q.reshape(B, S, H, Dh).transpose(0, 2, 1, 3)
        K = K.reshape(B, S, H, Dh).transpose(0, 2, 1, 3)
        V = V.reshape(B, S, H, Dh).transpose(0, 2, 1, 3)
        Q, K = (_rope(Q), _rope(K))
        scores = jnp.einsum('bhqd,bhkd->bhqk', Q, K) / jnp.sqrt(jnp.float32(Dh))
        probs = jax.nn.softmax(scores, axis=-1)
        ctx = jnp.einsum('bhqk,bhkd->bhqd', probs, V)
        ctx = ctx.transpose(0, 2, 1, 3).reshape(B, S, D)
        out = jnp.einsum('bsd,df->bsf', ctx, W_out)
        return out + X

    def _L0_ffn_ref(hidden_states, gate_w, bias, w_gate, w_up, w_down, ws_gate, ws_up, ws_down):
        import jax, jax.numpy as jnp
        import numpy as np
        E, K, H, F = (64, 6, 512, 192)
        G, KG = (8, 4)
        SHARED_F = 192
        SCALE = 2.5
        T = 2 * 256
        CAP = 2 * (T * K // E)

        def _grouped_topk(logits, bias):
            scores = jax.nn.sigmoid(logits.astype(jnp.float32))
            scores_b = scores + bias[None, :]
            gs = scores_b.reshape(-1, G, E // G)
            group_scores = jnp.sum(jax.lax.top_k(gs, 2)[0], axis=-1)
            gidx = jax.lax.top_k(group_scores, KG)[1]
            rows = jnp.arange(group_scores.shape[0])[:, None]
            group_mask = jnp.zeros_like(group_scores).at[rows, gidx].set(1.0)
            score_mask = jnp.repeat(group_mask, E // G, axis=-1) > 0
            tmp = jnp.where(score_mask, scores_b, -jnp.inf)
            topk_ids = jax.lax.top_k(tmp, K)[1]
            topk_w = jnp.take_along_axis(scores, topk_ids, axis=-1)
            topk_w = topk_w / jnp.sum(topk_w, axis=-1, keepdims=True)
            return (topk_w * SCALE, topk_ids)

        def _routed_moe(x, topk_w, topk_ids, w_gate, w_up, w_down):
            Tn = x.shape[0]
            flat_e = topk_ids.reshape(-1)
            order = jnp.argsort(flat_e)
            se = flat_e[order]
            pos = jnp.arange(Tn * K) - jnp.searchsorted(se, se, side='left')
            tok = order // K
            valid = pos < CAP
            slot = jnp.where(valid, pos, CAP)
            buf = jnp.zeros((E, CAP + 1, H), x.dtype).at[se, slot].set(x[tok])[:, :CAP]
            h = jax.nn.silu(jnp.einsum('ech,ehf->ecf', buf, w_gate)) * jnp.einsum('ech,ehf->ecf', buf, w_up)
            out = jnp.einsum('ecf,efh->ech', h, w_down)
            gathered = out[se, jnp.minimum(pos, CAP - 1)] * valid.astype(x.dtype)[:, None]
            w = topk_w.reshape(-1)[order].astype(x.dtype)[:, None]
            return jax.ops.segment_sum(gathered * w, tok, num_segments=Tn)
        orig_shape = hidden_states.shape
        x = hidden_states.reshape(-1, H)
        router_logits = x @ gate_w
        topk_w, topk_ids = _grouped_topk(router_logits, bias)
        y = _routed_moe(x, topk_w, topk_ids, w_gate, w_up, w_down)
        shared = jax.nn.silu(x @ ws_gate) * (x @ ws_up) @ ws_down
        return (y + shared).reshape(orig_shape)
    x = L0_attn_X
    x = x + 0.5 * _L0_ffn_ref(_layernorm(x, axis=-1), L0_ffn_gate_w, L0_ffn_bias, L0_ffn_w_gate, L0_ffn_w_up, L0_ffn_w_down, L0_ffn_ws_gate, L0_ffn_ws_up, L0_ffn_ws_down)
    x = x + _L0_attn_ref(_layernorm(x, axis=-1), L0_attn_ln_w, L0_attn_ln_b, L0_attn_W_in, L0_attn_W_out)
    x = x + 0.5 * _L0_ffn_ref(_layernorm(x, axis=-1), L0_ffn_gate_w, L0_ffn_bias, L0_ffn_w_gate, L0_ffn_w_up, L0_ffn_w_down, L0_ffn_ws_gate, L0_ffn_ws_up, L0_ffn_ws_down)
    return x

_drawn_inputs = setup_inputs


def setup_inputs(seed=0):
    import zlib

    import numpy as np

    out = dict(_drawn_inputs(seed))
    spreads = {'L0_attn_ln_w': (1.0, 0.6), 'L0_attn_ln_b': (0.0, 0.79)}
    factors = {'L0_attn_W_in': 4.945,
     'L0_attn_W_out': 5.042,
     'L0_ffn_gate_w': 3.627,
     'L0_ffn_bias': 6.326,
     'L0_ffn_w_gate': 3.534,
     'L0_ffn_w_up': 3.455,
     'L0_ffn_w_down': 3.468}
    for name, (base, spread) in spreads.items():
        noise = np.random.default_rng([zlib.crc32(name.encode()), seed]).standard_normal(out[name].shape)
        drawn = base * np.exp(spread * noise) if base else spread * noise
        out[name] = jnp.asarray(drawn.astype(out[name].dtype))
    for name, factor in factors.items():
        out[name] = (out[name] * factor).astype(out[name].dtype)
    return out
```

```python
from contextlib import ExitStack

import concourse.bass as bass
import numpy as np
from concourse import mybir

F32 = mybir.dt.float32
F32R = mybir.dt.float32r
BF16 = mybir.dt.bfloat16
U32 = mybir.dt.uint32
ALU = mybir.AluOpType
ACT = mybir.ActivationFunctionType
AX = mybir.AxisListType.X

D = 512
T = 2048
NT = 16
B = 4
S = 512
NH = 16
DH = 32
E = 64
K = 6
F = 192
FH = 96
CAP = 96
NG = 8
KG = 4
ROW = D + E
EPS = 1e-5
BIG = 3.0e38
SM = float(1.0 / np.sqrt(np.float32(DH)))

C_ID, C_UT, C_LM, C_IE, C_RB, C_TK, C_N = 0, 128, 256, 320, 384, 448, 464


def shape_constants():
    c = np.zeros((128, C_N), np.float32)
    p = np.arange(128)
    c[:, C_ID:C_ID + 128] = np.eye(128)
    c[:, C_UT:C_UT + 128] = p[:, None] < np.arange(128)[None, :]
    g = np.arange(NG)
    c[:, C_LM:C_LM + 64] = (g[None, :] < g[:, None]).astype(np.float32).reshape(1, 64)
    c[:, C_IE:C_IE + 64] = np.arange(E)[None, :]
    c[:, C_RB:C_RB + 64] = E * CAP - CAP * np.arange(E)[None, :]
    c[:, C_TK:C_TK + 16] = T - (np.arange(NT)[None, :] * 128 + p[:, None])
    rot = DH // 2
    inv = (np.float32(1.0) / np.float32(10000.0) ** (np.arange(0, rot, 2, dtype=np.float32) / np.float32(rot))).astype(np.float32)
    ang = np.repeat((np.arange(S, dtype=np.float32)[:, None] * inv[None, :]).astype(np.float32), 2, axis=-1)
    r = np.zeros((DH, 2, S), np.float32)
    r[:, 0, :] = 1.0
    r[:rot, 0, :] = np.cos(ang).T
    r[:rot, 1, :] = np.sin(ang).T * np.where(np.arange(rot) % 2 == 0, -1.0, 1.0)[:, None]
    return c, np.tile(r, (4, 1, 1)).astype(np.float32)


class Queues:

    def __init__(self, nc, ctx):
        self.items = {n: [] for n in ("pe", "act", "dve", "pool", "sp")}
        self.sem = {n: ctx.enter_context(nc.semaphore("done_" + n)) for n in self.items}
        self.count = dict.fromkeys(self.items, 0)
        self.dma_count = {}
        self.dma_last = {}

    def op(self, eng, fn, *waits):
        self.count[eng] += 1
        self.items[eng].append((fn, waits, self.sem[eng], 1))
        return ("done_" + eng, self.sem[eng], self.count[eng])

    def quiet(self, eng, fn, *waits):
        self.items[eng].append((fn, waits, None, 0))

    def dma(self, eng, name, sem, fn, *waits):
        self.dma_count[name] = self.dma_count.get(name, 0) + 16
        self.items[eng].append((fn, waits, sem, 16))
        self.dma_last[name] = (name, sem, self.dma_count[name])
        return self.dma_last[name]

    def wait(self, eng, *waits):
        self.items[eng].append((None, waits, None, 0))

    def all_done(self):
        return [("done_" + n, self.sem[n], v) for n, v in self.count.items() if v] + list(self.dma_last.values())

    def emit(self, eng, e):
        seen = {}
        for fn, waits, sem, by in self.items[eng]:
            for w in waits:
                for name, s, v in (w if isinstance(w, list) else [w]):
                    if seen.get(name, 0) < v:
                        e.wait_ge(s, v)
                        seen[name] = v
            if fn is not None:
                ins = fn(e)
                if sem is not None:
                    ins.then_inc(sem, by)


def macaron_kernel(nc, X_in, ln_w, ln_b, W_in, W_out, gate_w, bias, w_gate, w_up, w_down,
                   ws_gate, ws_up, ws_down, consts, rope, out):
    x_rows = X_in.rearrange("b s d -> (b s) d")
    o_rows = out.rearrange("b s d -> (b s) d")

    with ExitStack() as ctx:
        base = 16 * 1024 + 128
        names = {}

        def at(name, off, shape, dt=F32):
            names[name] = names.get(name, 0) + 1
            return nc.alloc_sbuf_tensor_at(f"{name}_{names[name]}", shape, dt, offset=base + off)

        def sem(name):
            return ctx.enter_context(nc.semaphore(name))

        KB = 1024
        X = at("X", 0, [128, NT, D])
        cst = at("cst", 32 * KB, [128, C_N])
        utb = at("utb", 34 * KB, [128, 128], BF16)
        onb = at("onb", 34 * KB + 256, [128, 128], BF16)
        biasb = at("biasb", 34 * KB + 512, [128, E])
        lnw = at("lnw", 34 * KB + 768, [128, 4])
        lnb = at("lnb", 34 * KB + 800, [128, 4])
        gw = at("gw", 35 * KB, [128, 4, E])
        wsgu = at("wsgu", 36 * KB, [128, 4, 2, F])
        wsd = at("wsd", 42 * KB, [128, 2, D])
        A0 = 46 * KB
        ident = cst[:, C_ID:C_ID + 128]

        ps = [ctx.enter_context(nc.psum_tensor(f"ps{i}", [128, 2, 512], F32)) for i in range(4)]

        def bank(i):
            return ps[i // 2][:, i % 2, :]

        q = Queues(nc, ctx)
        op, dma = q.op, q.dma

        s_x = [sem(f"s_x{g}") for g in range(4)]
        s_c = sem("s_c")
        s_ln = sem("s_ln")
        s_fw = sem("s_fw")
        s_aw = sem("s_aw")

        tx = [dma("sp", f"x{g}", s_x[g], lambda e, g=g: e.dma_start(
            X[:, 4 * g:4 * g + 4, :], x_rows[512 * g:512 * g + 512, :].rearrange("(i p) d -> p i d", p=128)))
            for g in range(4)]
        tc = dma("act", "c", s_c, lambda e: e.dma_start(cst[:, :], consts))
        tc = dma("act", "c", s_c, lambda e: e.dma_start(biasb[:, :], bias.partition_broadcast(128)))
        tc = dma("act", "c", s_c, lambda e: e.dma_start(gw[:, :, :], gate_w.rearrange("(p c) n -> p c n", c=4)))
        tfw = dma("act", "fw", s_fw, lambda e: e.dma_start(wsgu[:, :, 0, :], ws_gate.rearrange("(p c) n -> p c n", c=4)))
        tfw = dma("act", "fw", s_fw, lambda e: e.dma_start(wsgu[:, :, 1, :], ws_up.rearrange("(p c) n -> p c n", c=4)))
        tfw = dma("act", "fw", s_fw, lambda e: e.dma_start(wsd[0:FH, :, :], ws_down.rearrange("(c p) n -> p c n", c=2)))
        tln = dma("act", "ln", s_ln, lambda e: e.dma_start(lnw[:, :], ln_w.rearrange("(p c) -> p c", c=4)))
        tln = dma("act", "ln", s_ln, lambda e: e.dma_start(lnb[:, :], ln_b.rearrange("(p c) -> p c", c=4)))
        op("dve", lambda e: e.tensor_copy(utb[:, :], cst[:, C_UT:C_UT + 128]), tc)
        tcb = op("dve", lambda e: e.memset(onb[:, :], 1.0))

        t_x = [tx[i // 4] for i in range(NT)]

        def rstd(src_var, ve, sq, r, t, wait):
            a = op("dve", lambda e: e.tensor_scalar(ve, src_var, EPS, None, ALU.add), wait)
            b = op("act", lambda e: e.activation(sq, ve, ACT.Sqrt), a)
            c = op("dve", lambda e: e.reciprocal(r, sq), b)
            c = op("dve", lambda e: e.tensor_tensor(t, r, r, ALU.mult), c)
            c = op("dve", lambda e: e.tensor_tensor(t, t, ve, ALU.mult), c)
            c = op("dve", lambda e: e.tensor_scalar(t, t, -0.5, 1.5, ALU.mult, ALU.add), c)
            return op("dve", lambda e: e.tensor_tensor(r, r, t, ALU.mult), c)

        def ffn(n, t_x):
            NR = 7
            ring = [(at("gu", A0 + r * 10 * KB, [128, 4, 2, F]), at("wd", A0 + r * 10 * KB + 6 * KB, [FH, 2, D]))
                    for r in range(NR)]
            A1 = A0 + 70 * KB
            xnT = at("xnT", A1, [128, 4, T])
            XN = at("XN", A1 + 32 * KB, [128, 4, D])
            buf = [at("buf", A1 + j * 2304, [CAP, ROW]) for j in range(4)]
            o = A1 + 4 * 2304
            bufT = [at("bufT", o + j * 1536, [128, 4, CAP]) for j in range(2)]
            sg = [at("sg", o + 3072 + j * 768, [FH, 2, CAP]) for j in range(2)]
            hT = [at("hT", o + 4608 + j * 768, [FH, 2, CAP]) for j in range(2)]
            osb = [at("osb", o + 6144 + j * 2048, [CAP, D]) for j in range(3)]
            A2 = A1 + 40 * KB
            R = [at(f"R{j}", A2 + 4 * KB * j, [128, NT, E]) for j in range(7)]
            G = [at("G", A2 + 12 * KB * j, [128, K, D]) for j in range(2)]
            SELb = at("SELb", A2 + 28 * KB, [128, NT, E], BF16)
            CUMb = at("CUMb", A2 + 30 * KB, [128, NT, E], BF16)
            keyT = at("keyT", A2 + 32 * KB, [128, T // 2])
            sgs = at("sgs", A2 + 36 * KB, [FH, 2, S])
            hTs = at("hTs", A2 + 40 * KB, [FH, 2, S])
            A3 = A2 + 44 * KB
            BS = at("BS", A3, [128, NT, 6])
            MV = at("MV", A3 + 384, [128, NT, 2])
            VE = at("VE", A3 + 512, [128, NT])
            SQ = at("SQ", A3 + 576, [128, NT])
            RS = at("RS", A3 + 640, [128, NT])
            TM = at("TM", A3 + 704, [128, NT])
            V8 = at("V8", A3 + 768, [128, NT, 8])
            I8 = at("I8", A3 + 1280, [128, NT, 8], U32)
            SLOT = at("SLOT", A3 + 1792, [128, NT, 8], U32)
            i6 = at("i6", A3 + 2304, [128, NT])
            den = at("den", A3 + 2368, [128, NT])
            lst = at("lst", A3 + 2432, [128, CAP])
            cand = at("cand", A3 + 2816, [E, 2 * CAP])
            first = at("first", A3 + 3584, [E, CAP])
            tok = at("tok", A3 + 3968, [CAP, E], U32)
            tokf = at("tokf", A3 + 4224, [CAP, E])
            assert A3 + 4480 <= 207 * KB

            xn_d = nc.dram_tensor(f"xn_d{n}", [T, ROW], F32, kind="Internal").ap()
            out_d = nc.dram_tensor(f"out_d{n}", [E * CAP, D], F32, kind="Internal").ap()
            s_ring = [sem(f"s_ring{n}_{r}") for r in range(NR)]
            s_xn = [sem(f"s_xn{n}_{r}") for r in range(4)]
            s_w = sem(f"s_w{n}")
            s_buf = [sem(f"s_buf{n}_{r}") for r in range(4)]
            s_out = [sem(f"s_out{n}_{r}") for r in range(3)]
            s_g = [sem(f"s_g{n}_{r}") for r in range(2)]

            def load(x, *waits):
                gu, wd = ring[x % NR]
                nm, s = f"ring{n}_{x % NR}", s_ring[x % NR]
                dma("sp", nm, s, lambda e: e.dma_start(gu[:, :, 0, :], w_gate[x].rearrange("(p c) f -> p c f", c=4)), *waits)
                dma("sp", nm, s, lambda e: e.dma_start(gu[:, :, 1, :], w_up[x].rearrange("(p c) f -> p c f", c=4)))
                return dma("sp", nm, s, lambda e: e.dma_start(wd[:, :, :], w_down[x].rearrange("(c p) h -> p c h", c=2)))

            t_ring = {x: load(x) for x in range(NR)}

            tb, t_evT, t_lg, t_xnd = {}, {}, {}, {}
            for g in range(4):
                tiles = range(4 * g, 4 * g + 4)
                for i in tiles:
                    tb[i] = op("dve", lambda e, i=i: e.bn_stats(BS[:, i, :], X[:, i, :]), t_x[i])
                for i in tiles:
                    tb[i] = op("dve", lambda e, i=i: e.bn_aggr(MV[:, i, :], BS[:, i, :]), tb[i])
                gs = slice(4 * g, 4 * g + 4)
                tr = rstd(MV[:, gs, 1], VE[:, gs], SQ[:, gs], RS[:, gs], TM[:, gs], tb[4 * g + 3])
                for i in tiles:
                    w = [t_evT[i - 4], t_xnd[i - 4]] if i >= 4 else []
                    tn = op("dve", lambda e, i=i: e.tensor_scalar(XN[:, i % 4, :], X[:, i, :], MV[:, i, 0:1], RS[:, i:i + 1],
                                                                  ALU.subtract, ALU.mult), tr, *w)
                    t_xnd[i] = dma("act", f"xn{n}_{i % 4}", s_xn[i % 4], lambda e, i=i: e.dma_start(
                        xn_d[128 * i:128 * i + 128, 0:D], XN[:, i % 4, :]), tn)
                    w = [t_evT[i - 2]] if i >= 2 else []
                    for c in range(4):
                        tt = op("pe", lambda e, i=i, c=c: e.transpose(bank(i % 2)[:, 128 * c:128 * c + 128], XN[:, i % 4, c:D:4], ident),
                                tn, tc, *w)
                    t_evT[i] = op("act", lambda e, i=i: e.copy(xnT[:, :, 128 * i:128 * i + 128],
                                                               bank(i % 2).rearrange("p (c t) -> p c t", c=4)), tt)
                    for c in range(4):
                        t_lg[i] = op("pe", lambda e, i=i, c=c: e.matmul(
                            bank(2 + i // 8)[:, 64 * (i % 8):64 * (i % 8) + 64],
                            xnT[:, c, 128 * i:128 * i + 128], gw[:, c, :], start=(c == 0), stop=(c == 3)), t_evT[i])

            t_hs, t_up, t_sh, t_dn, t_shc = {}, {}, {}, {}, {}

            def shared_up(gq):
                w = [t_hs[gq - 1]] if gq else []
                for j in range(4):
                    for c in range(4):
                        t_up[gq] = op("pe", lambda e, j=j, c=c: e.matmul(
                            bank(4 + j)[0:FH, :], wsgu[:, c, j // 2, FH * (j % 2):FH * (j % 2) + FH],
                            xnT[:, c, S * gq:S * gq + S], start=(c == 0), stop=(c == 3)), tfw, t_evT[4 * gq + 3], *w)

            def shared_act(gq):
                w = [t_hs[gq - 1]] if gq else []
                a = op("act", lambda e: e.activation(sgs[:, :, :], ps[2][0:FH, :, :], ACT.Silu), t_up[gq], *w)
                w = [t_dn[gq - 1]] if gq else []
                t_hs[gq] = op("dve", lambda e: e.tensor_tensor(hTs[:, :, :], sgs[:, :, :], ps[3][0:FH, :, :], ALU.mult), a, *w)

            def shared_down(gq):
                for j in range(4):
                    i = 4 * gq + j
                    w = [t_shc[i - 2]] if i >= 2 else [t_evT[NT - 1]]
                    for h in range(2):
                        t_dn[gq] = op("pe", lambda e, j=j, i=i, h=h: e.matmul(
                            bank(i % 2), hTs[:, h, 128 * j:128 * j + 128], wsd[0:FH, h, :],
                            start=(h == 0), stop=(h == 1)), t_hs[gq], *w)
                    w = [t_sh[i - 4]] if i >= 4 else [t_xnd[NT - 4 + i]]
                    t_shc[i] = op("act", lambda e, i=i: e.activation(XN[:, i % 4, :], bank(i % 2), ACT.Copy, scale=0.5), t_dn[gq], *w)
                    t_sh[i] = op("pool", lambda e, i=i: e.tensor_tensor(X[:, i, :], X[:, i, :], XN[:, i % 4, :], ALU.add), t_shc[i])

            SC, SB, P1, P2, SEL, W, P3 = [r[:, :, :] for r in R]
            flat = lambda ap: ap.rearrange("p i e -> p (i e)")
            grp = lambda ap: ap.rearrange("p i (g j) -> p (i g) j", j=8)
            bE = lambda ap: ap.unsqueeze(2).to_broadcast([128, NT, E])
            cE = lambda o: cst[:, o:o + 64].unsqueeze(1).to_broadcast([128, NT, E])
            dv = lambda fn, *w: op("dve", fn, *w)
            TT = lambda o, a, b, f: (lambda e: e.tensor_tensor(o, a, b, f))

            shared_up(0)
            t_sc = op("act", lambda e: e.activation(SC.rearrange("p (a i) e -> p a (i e)", a=2), ps[1][:, :, :], ACT.Sigmoid), t_lg[NT - 1])
            shared_act(0)
            shared_up(1)
            shared_down(0)
            t = dv(TT(SB, SC, biasb[:, :].unsqueeze(1).to_broadcast([128, NT, E]), ALU.add), t_sc, tc)
            s8 = grp(SB)
            part = lambda ap, o, m, j: flat(ap)[:, o:o + m * j].rearrange("p (m j) -> p m j", j=j)
            h1, l1 = part(P1, 0, 128, 4), part(P1, 512, 128, 4)
            h2, l2, u2 = part(P2, 0, 128, 2), part(P2, 256, 128, 2), part(P2, 512, 128, 2)
            h3, l3, u3, gsum, rank, msk, neg = (flat(P3)[:, 128 * j:128 * j + 128] for j in range(7))
            dv(TT(h1, s8[:, :, 0::2], s8[:, :, 1::2], ALU.max), t)
            t = dv(TT(l1, s8[:, :, 0::2], s8[:, :, 1::2], ALU.min), t)
            dv(TT(h2, h1[:, :, 0::2], h1[:, :, 1::2], ALU.max), t)
            dv(TT(l2, h1[:, :, 0::2], h1[:, :, 1::2], ALU.min), t)
            t = dv(TT(u2, l1[:, :, 0::2], l1[:, :, 1::2], ALU.max), t)
            t = dv(TT(l2, l2, u2, ALU.max), t)
            dv(TT(h3, h2[:, :, 0], h2[:, :, 1], ALU.max), t)
            dv(TT(l3, h2[:, :, 0], h2[:, :, 1], ALU.min), t)
            t = dv(TT(u3, l2[:, :, 0], l2[:, :, 1], ALU.max), t)
            t = dv(TT(l3, l3, u3, ALU.max), t)
            t = dv(TT(gsum, h3, l3, ALU.add), t)
            G3 = gsum.rearrange("p (i g) -> p i g", g=NG)
            ga = G3.unsqueeze(2).to_broadcast([128, NT, NG, NG])
            gb = G3.unsqueeze(3).to_broadcast([128, NT, NG, NG])
            r4 = lambda ap: ap.rearrange("p i (g j) -> p i g j", j=NG)
            dv(TT(r4(P1), ga, gb, ALU.is_gt), t)
            t = dv(TT(r4(P2), ga, gb, ALU.is_equal), t)
            t = dv(TT(P2, P2, cE(C_LM), ALU.mult), t)
            t = dv(TT(P1, P1, P2, ALU.add), t)
            t = dv(lambda e: e.tensor_reduce(rank, grp(P1), AX, ALU.add), t)
            t = dv(lambda e: e.tensor_scalar(msk, rank, float(KG), None, ALU.is_lt), t)
            t = dv(lambda e: e.tensor_scalar(neg, msk, BIG, -BIG, ALU.mult, ALU.add), t)
            bg = lambda ap: ap.unsqueeze(2).to_broadcast([128, 128, 8])
            t = dv(TT(grp(P1), s8, bg(msk), ALU.mult), t)
            t = dv(TT(grp(P1), grp(P1), bg(neg), ALU.add), t)
            shared_act(1)
            for i in range(NT):
                tv = dv(lambda e, i=i: e.max(V8[:, i, :], P1[:, i, :]), t)
            for i in range(NT):
                ti = dv(lambda e, i=i: e.max_index(I8[:, i, :], V8[:, i, :], P1[:, i, :]), tv)
            t = dv(lambda e: e.tensor_copy(i6[:, :], I8[:, :, K - 1]), ti)
            dv(TT(P2, cE(C_IE), bE(i6[:, :]), ALU.is_le), t)
            t = dv(TT(SEL, P1, bE(V8[:, :, K - 1]), ALU.is_equal), t)
            t3 = dv(TT(P3, P1, bE(V8[:, :, K - 1]), ALU.is_gt), t)
            t = dv(TT(P2, P2, SEL, ALU.mult), t)
            t_sel = dv(TT(SEL, P2, P3, ALU.add), t, t3)
            t_key = dv(TT(flat(P1).rearrange("p (i a e) -> p a i e", a=2, e=E), SEL.rearrange("p (a i) e -> p a i e", a=2),
                          cst[:, C_TK:C_TK + 16].rearrange("p (a i) -> p a i", a=2).unsqueeze(3).to_broadcast([128, 2, 8, E]),
                          ALU.mult), t_sel)
            for i in range(8):
                tp = op("pe", lambda e, i=i: e.transpose(bank(2 + i // 4)[:, 128 * (i % 4):128 * (i % 4) + 128],
                                                         flat(P1)[:, 128 * i:128 * i + 128], ident), t_key, t_sc)
            shared_up(2)
            shared_down(1)
            t = dv(TT(P2, SC, SEL, ALU.mult), t_sel)
            t = dv(lambda e: e.tensor_reduce(den[:, :], P2, AX, ALU.add), t)
            t = dv(lambda e: e.reciprocal(den[:, :], den[:, :]), t)
            t = dv(lambda e: e.scalar_tensor_tensor(out=W, in0=P2, scalar=1.25, in1=bE(den[:, :]), op0=ALU.mult, op1=ALU.mult), t)
            t_wd = dma("act", f"w{n}", s_w, lambda e: e.dma_start(xn_d[:, D:ROW].rearrange("(i p) e -> p i e", p=128), W), t)
            t_kT = dv(lambda e: e.tensor_copy(keyT[:, :].rearrange("p (a b) -> p a b", a=2), ps[1][:, :, :]), tp)
            shared_act(2)
            t = t_kT
            for r in range(CAP // 8):
                t = dv(lambda e, r=r: e.max(lst[:, 8 * r:8 * r + 8], keyT[:, :]), t)
                if r < CAP // 8 - 1:
                    t = dv(lambda e, r=r: e.match_replace(keyT[:, :], lst[:, 8 * r:8 * r + 8], keyT[:, :], 0.0), t)
                if r == 5:
                    shared_up(3)
                    shared_down(2)
                    shared_act(3)
            dv(lambda e: e.tensor_copy(cand[:, 0:CAP], lst[0:E, :]), t)
            t = dv(lambda e: e.tensor_copy(cand[:, CAP:2 * CAP], lst[E:128, :]), t)
            for r in range(CAP // 8):
                t = dv(lambda e, r=r: e.max(first[:, 8 * r:8 * r + 8], cand[:, :]), t)
                if r < CAP // 8 - 1:
                    t = dv(lambda e, r=r: e.match_replace(cand[:, :], first[:, 8 * r:8 * r + 8], cand[:, :], 0.0), t)
            tp = op("pe", lambda e: e.transpose(bank(2)[0:CAP, 0:E], first[:, :], cst[0:E, C_ID:C_ID + E]), t, t_kT)
            t = dv(lambda e: e.tensor_scalar(tokf[:, :], bank(2)[0:CAP, 0:E], -1.0, float(T), ALU.mult, ALU.add), tp)
            t_tok = dv(lambda e: e.tensor_scalar(tok[:, :], tokf[:, :], float(T - 1), None, ALU.min), t)
            shared_down(3)
            t_sb = dv(lambda e: e.tensor_copy(SELb[:, :, :], SEL), t_sel)
            t = dv(lambda e: e.memset(CUMb[:, 0, :], 0.0))
            for i in range(1, NT):
                t = dv(lambda e, i=i: e.tensor_tensor(CUMb[:, i, :], CUMb[:, i - 1, :], SELb[:, i - 1, :], ALU.add), t, t_sb)
            fb = lambda ap, h: ap[:, 8 * h:8 * h + 8, :].rearrange("p i e -> p (i e)")
            for h in range(2):
                op("pe", lambda e, h=h: e.matmul(bank(2 + h), utb[:, :], fb(SELb, h), start=True, stop=False), t, t_tok, tcb)
                tp = op("pe", lambda e, h=h: e.matmul(bank(2 + h), onb[:, :], fb(CUMb, h), start=False, stop=True), t)
            pos = ps[1][:, :, :].rearrange("p a (i e) -> p (a i) e", e=E)
            t = dv(TT(P1, cE(C_RB), pos, ALU.subtract), tp)
            t2 = dv(lambda e: e.scalar_tensor_tensor(out=flat(P2).rearrange("p (a n) -> p a n", a=2), in0=ps[1][:, :, :], scalar=float(CAP),
                                                     in1=flat(SEL).rearrange("p (a n) -> p a n", a=2), op0=ALU.is_lt, op1=ALU.mult), tp)
            t_pos = t2
            t = dv(TT(P1, P1, P2, ALU.mult), t2)
            for i in range(NT):
                tv = dv(lambda e, i=i: e.max(V8[:, i, :], P1[:, i, :]), t)
            t_slot = dv(lambda e: e.tensor_scalar(SLOT[:, :, :], V8[:, :, :], -1.0, float(E * CAP), ALU.mult, ALU.add), tv)

            t_buf, t_bT, t_gu, t_h, t_d, t_ev, t_out = {}, {}, {}, {}, {}, {}, {}

            def gather(x):
                w = [t_ev[x - 4]] if x >= 4 else [t_tok, t_wd, t_up[3]] + [t_xnd[i] for i in range(NT - 4, NT)]
                t_buf[x] = dma("pool", f"buf{n}_{x % 4}", s_buf[x % 4], lambda e: e.indirect_dma_start(
                    out=buf[x % 4][:, :], out_offset=None, in_=xn_d, in_offset=bass.IndirectOffsetOnAxis(ap=tok[:, x:x + 1], axis=0),
                    bounds_check=T - 1, oob_is_err=False), *w)

            for x in range(4):
                gather(x)
            for st in range(E + 2):
                x = st
                if x < E:
                    w = [t_bT[x - 2]] if x >= 2 else [t_shc[NT - 1]]
                    for c in range(4):
                        tt = op("pe", lambda e, x=x, c=c: e.transpose(bank(x % 2)[:, CAP * c:CAP * c + CAP],
                                                                      buf[x % 4][:, c:D:4], cst[0:CAP, C_ID:C_ID + CAP]), t_buf[x], *w)
                    w = [t_gu[x - 2]] if x >= 2 else []
                    t_bT[x] = op("act", lambda e, x=x: e.copy(bufT[x % 2][:, :, :], bank(x % 2)[:, 0:4 * CAP].rearrange("p (c t) -> p c t", c=4)), tt, *w)
                x = st - 1
                if 0 <= x < E:
                    gu, wd = ring[x % NR]
                    w = [t_h[x - 2]] if x >= 2 else [t_pos]
                    for j in range(4):
                        for c in range(4):
                            t_gu[x] = op("pe", lambda e, x=x, gu=gu, j=j, c=c: e.matmul(
                                bank(2 + x % 2)[0:FH, CAP * j:CAP * j + CAP], gu[:, c, j // 2, FH * (j % 2):FH * (j % 2) + FH],
                                bufT[x % 2][:, c, :], start=(c == 0), stop=(c == 3)), t_bT[x], t_ring[x], *w)
                    w = [t_h[x - 2]] if x >= 2 else []
                    a = op("act", lambda e, x=x: e.activation(sg[x % 2][:, :, :].rearrange("p a b -> p (a b)"),
                                                              bank(2 + x % 2)[0:FH, 0:2 * CAP], ACT.Silu), t_gu[x], *w)
                    w = [t_d[x - 2]] if x >= 2 else []
                    t_h[x] = op("dve", lambda e, x=x: e.tensor_tensor(
                        hT[x % 2][:, :, :].rearrange("p a b -> p (a b)"), sg[x % 2][:, :, :].rearrange("p a b -> p (a b)"),
                        bank(2 + x % 2)[0:FH, 2 * CAP:4 * CAP], ALU.mult), a, *w)
                x = st - 2
                if 0 <= x < E:
                    gu, wd = ring[x % NR]
                    w = [t_ev[x - 2]] if x >= 2 else [t_hs[3]]
                    for h in range(2):
                        t_d[x] = op("pe", lambda e, x=x, wd=wd, h=h: e.matmul(bank(4 + x % 2)[0:CAP, :], hT[x % 2][:, h, :], wd[:, h, :],
                                                                            start=(h == 0), stop=(h == 1)), t_h[x], *w)
                    w = [t_out[x - 3]] if x >= 3 else []
                    t_ev[x] = op("dve", lambda e, x=x: e.tensor_scalar(osb[x % 3][:, :], bank(4 + x % 2)[0:CAP, :],
                                                                       buf[x % 4][:, D + x:D + x + 1], None, ALU.mult), t_d[x], *w)
                    t_out[x] = dma("sp", f"out{n}_{x % 3}", s_out[x % 3], lambda e, x=x: e.dma_start(
                        out_d[CAP * x:CAP * x + CAP, :], osb[x % 3][:, :]), t_ev[x])
                    if x + NR < E:
                        t_ring[x + NR] = load(x + NR, t_d[x])
                    if x + 4 < E:
                        gather(x + 4)

            t_cx = {}
            for i in range(NT):
                g = G[i % 2]
                w = [t_cx[i - 2]] if i >= 2 else [t_slot]
                tm = op("dve", lambda e, g=g: e.memset(g[:, :, :], 0.0), *w)
                for k in range(K):
                    tg = dma("pool", f"g{n}_{i % 2}", s_g[i % 2], lambda e, g=g, i=i, k=k: e.indirect_dma_start(
                        out=g[:, k, :], out_offset=None, in_=out_d, in_offset=bass.IndirectOffsetOnAxis(ap=SLOT[:, i, k:k + 1], axis=0),
                        bounds_check=E * CAP - 1, oob_is_err=False), tm, *[t_out[x] for x in range(E - 3, E)])
                t = op("dve", lambda e, g=g: e.tensor_tensor(g[:, 0::2, :], g[:, 0::2, :], g[:, 1::2, :], ALU.add), tg)
                t = op("dve", lambda e, g=g: e.tensor_tensor(g[:, 0, :], g[:, 0, :], g[:, 2, :], ALU.add), t)
                t = op("dve", lambda e, g=g: e.tensor_tensor(g[:, 0, :], g[:, 0, :], g[:, 4, :], ALU.add), t)
                t_cx[i] = op("dve", lambda e, g=g, i=i: e.tensor_tensor(X[:, i, :], X[:, i, :], g[:, 0, :], ALU.add), t, t_sh[i])
            return [t_cx[i] for i in range(NT)]

        def phase():
            done = q.all_done()
            for n in q.items:
                q.wait(n, done)

        def attention(t_x):
            win = at("win", A0, [128, 4, 3 * D])
            wout = at("wout", A0 + 24 * KB, [128, 4, D])
            rp = at("rp", A0 + 32 * KB, [128, 2, S])
            xT = at("xT", A0 + 36 * KB, [128, 4, S])
            Z = at("Z", A0 + 44 * KB, [128, 2, D])
            ZH = at("ZH", A0 + 48 * KB, [128, 2, D])
            V = at("V", A0 + 52 * KB, [128, 4, NH, 64])
            HI = at("HI", A0 + 68 * KB, [128, 4, S], F32R)
            LO = at("LO", A0 + 76 * KB, [128, 4, S], F32R)
            Qs = at("Qs", A0 + 84 * KB, [98, 8, S], F32R)
            Ks = at("Ks", A0 + 100 * KB, [98, 8, S], F32R)
            PT = [at("PT", A0 + 116 * KB + 4 * KB * j, [128, 2, S]) for j in range(4)]
            cT = at("cT", A0 + 132 * KB, [128, 4, S])
            t1 = at("t1", A0 + 140 * KB, [128, 2, S])
            t2 = at("t2", A0 + 144 * KB, [128, 2, S])
            RD = at("RD", A0 + 148 * KB, [128, 2, S])
            Mx = at("Mx", A0 + 152 * KB, [128, 4, 8])
            mh = at("mh", A0 + 153 * KB, [8, 2, S], F32R)
            BS = at("BS", A0 + 157 * KB, [128, 4, 6])
            MV = at("MV", A0 + 157 * KB + 96, [128, 4, 2])
            sc4 = [at("sc4", A0 + 157 * KB + 128 + 32 * j, [128, 4]) for j in range(4)]
            s_st = sem("s_st")
            s_m = sem("s_m")

            taw = dma("sp", "aw", s_aw, lambda e: e.dma_start(win[:, :, :], W_in.rearrange("(p c) n -> p c n", c=4)))
            taw = dma("sp", "aw", s_aw, lambda e: e.dma_start(wout[:, :, :], W_out.rearrange("(c p) n -> p c n", c=4)))
            taw = dma("sp", "aw", s_aw, lambda e: e.dma_start(rp[:, :, :], rope))
            op("dve", lambda e: e.memset(V[:, :, :, 32:64], 1.0))
            t_one = op("dve", lambda e: e.memset(Ks[96:98, :, :].bitcast(F32), 1.0))

            mx = [None]
            st = {"ring01": [None, None], "xT": [], "V": [], "hilo": None, "stack": None, "t1": [None, None], "pt": [None] * 4,
                  "ctx": [None, None], "cT": [], "S": [None, None], "m": None, "Z": [None, None], "zh": [None, None], "mx": None}
            turn = [0]

            def take():
                j = turn[0] % 2
                turn[0] += 1
                return j, ([st["ring01"][j]] if st["ring01"][j] else [])

            w_ = lambda *xs: [x for x in xs if x]
            t_xo = {}

            def prepare(b):
                tb = {}
                VE, SQ, RS, TM = [a[:, :] for a in sc4]
                tr = None
                for j in range(4):
                    tb[j] = op("dve", lambda e, j=j: e.bn_stats(BS[:, j, :], X[:, 4 * b + j, :]), t_x[4 * b + j], *w_(st["mx"]))
                for j in range(4):
                    tb[j] = op("dve", lambda e, j=j: e.bn_aggr(MV[:, j, :], BS[:, j, :]), tb[j])
                tr = rstd(MV[:, :, 1], VE, SQ, RS, TM, tb[3])
                for j in range(4):
                    i = 4 * b + j
                    tz = op("dve", lambda e, i=i, j=j: e.tensor_scalar(Z[:, j % 2, :], X[:, i, :], MV[:, j, 0:1], RS[:, j:j + 1],
                                                                       ALU.subtract, ALU.mult), tr, *w_(st["Z"][j % 2]))
                    t_xo[i] = op("pool", lambda e, i=i, j=j: e.tensor_tensor(X[:, i, :], X[:, i, :], Z[:, j % 2, :], ALU.add), tz)
                    t = op("dve", lambda e, j=j: e.bn_stats(BS[:, j, :], Z[:, j % 2, :]), tz)
                    t = op("dve", lambda e, j=j: e.bn_aggr(MV[:, j, :], BS[:, j, :]), t)
                    t = rstd(MV[:, j:j + 1, 1], VE[:, j:j + 1], SQ[:, j:j + 1], RS[:, j:j + 1], TM[:, j:j + 1], t)
                    th = op("dve", lambda e, j=j: e.tensor_scalar(ZH[:, j % 2, :], Z[:, j % 2, :], MV[:, j, 0:1], RS[:, j:j + 1],
                                                                  ALU.subtract, ALU.mult), t, *w_(st["zh"][j % 2]))
                    st["mx"] = th
                    st["Z"][j % 2] = [th, t_xo[i]]
                    bk, w = take()
                    for c in range(4):
                        tt = op("pe", lambda e, j=j, c=c, bk=bk: e.transpose(bank(bk)[:, 128 * c:128 * c + 128], ZH[:, j % 2, c:D:4], ident), th, *w)
                    st["zh"][j % 2] = tt
                    for c in range(4):
                        te = op("act", lambda e, j=j, c=c, bk=bk: e.activation(
                            xT[:, c, 128 * j:128 * j + 128], bank(bk)[:, 128 * c:128 * c + 128], ACT.Identity,
                            bias=lnb[:, c:c + 1], scale=lnw[:, c:c + 1]), tt, tln, *st["xT"])
                    st["ring01"][bk] = te
                st["xTr"] = te
                rd = []
                for j in range(4):
                    bk, w = take()
                    for c in range(4):
                        tt = op("pe", lambda e, j=j, c=c, bk=bk: e.matmul(bank(bk), xT[:, c, 128 * j:128 * j + 128], win[:, c, 2 * D:3 * D],
                                                                          start=(c == 0), stop=(c == 3)), te, taw, *w)
                    tv = op("act", lambda e, j=j, bk=bk: e.copy(V[:, j, :, 0:32], bank(bk).rearrange("p (h d) -> p h d", d=DH)), tt, *st["V"])
                    st["ring01"][bk] = tv
                st["Vr"] = tv

            def project(b, hf):
                for ch in range(4):
                    col = D * (ch // 2) + 256 * hf + 128 * (ch % 2)
                    bk, w = take()
                    for c in range(4):
                        tp = op("pe", lambda e, c=c, bk=bk, col=col: e.matmul(bank(bk), win[:, c, col:col + 128], xT[:, c, :],
                                                                            start=(c == 0), stop=(c == 3)), st["xTr"], taw, *w)
                    y = ch % 2
                    w = w_(st["t1"][y])
                    a = op("dve", lambda e, bk=bk, y=y: e.stream_shuffle(t2[:, y, :], bank(bk), [i ^ 1 for i in range(32)]), tp, *w)
                    a = op("pool", lambda e, y=y: e.tensor_tensor(t2[:, y, :], t2[:, y, :], rp[:, 1, :], ALU.mult), a, taw)
                    d = op("dve", lambda e, bk=bk, y=y: e.tensor_tensor(t1[:, y, :], bank(bk), rp[:, 0, :], ALU.mult), tp, taw, *w)
                    st["ring01"][bk] = d
                    d = op("pool", lambda e, y=y: e.tensor_tensor(t1[:, y, :], t1[:, y, :], t2[:, y, :], ALU.add), d, a)
                    h = op("act", lambda e, y=y, ch=ch: e.copy(HI[:, ch, :], t1[:, y, :]), d, *w_(st["stack"]))
                    l = op("dve", lambda e, y=y, ch=ch: e.tensor_tensor(LO[:, ch, :], t1[:, y, :], HI[:, ch, :].bitcast(F32), ALU.subtract),
                           h, *w_(st["stack"]))
                    st["t1"][y] = l
                if hf == 1:
                    st["xT"] = [tp]
                st["hilo"] = l

            def stack():
                for dst, ch, parts in ((Qs, 0, (HI, HI, LO)), (Ks, 2, (HI, LO, HI))):
                    for s_, src in enumerate(parts):
                        for j in range(4):
                            t = dma("sp", "st", s_st, lambda e, dst=dst, ch=ch, s_=s_, src=src, j=j: e.dma_start(
                                dst[32 * s_:32 * s_ + 32, j::4, :].bitcast(F32), src[32 * j:32 * j + 32, ch:ch + 2, :].bitcast(F32)), st["hilo"], *w_(*st["S"]))
                st["stack"] = t

            def maxima():
                tm = {}
                for hl in range(8):
                    for p2 in range(2):
                        bk = 1 + (2 * hl + p2) % 2
                        for y in range(2):
                            qt = 2 * p2 + y
                            t = op("pe", lambda e, bk=bk, y=y, hl=hl, qt=qt: e.matmul(
                                ps[bk][:, y, :], Qs[0:96, hl, 128 * qt:128 * qt + 128], Ks[0:96, hl, :], start=True, stop=True),
                                st["stack"], *w_(st["S"][bk - 1]))
                        st["S"][bk - 1] = op("dve", lambda e, bk=bk, hl=hl, p2=p2: e.tensor_reduce(
                            Mx[:, 2 * p2:2 * p2 + 2, hl], ps[bk][:, :, :], AX, ALU.max, negate=True), t, *w_(st["m"]))
                return st["S"][1]

            def rows(tm):
                bk, w = take()
                for qt in range(4):
                    t = op("pe", lambda e, qt=qt, bk=bk: e.transpose(bank(bk)[0:8, 128 * qt:128 * qt + 128], Mx[:, qt, :], ident), tm, *w)
                st["m"] = t
                a = op("act", lambda e, bk=bk: e.copy(mh[:, 0, :], bank(bk)[0:8, :]), t, *w_(st.get("md")))
                d = op("dve", lambda e, bk=bk: e.tensor_tensor(mh[:, 1, :], bank(bk)[0:8, :], mh[:, 0, :].bitcast(F32), ALU.subtract), a)
                st["ring01"][bk] = d
                for j in range(2):
                    st["md"] = dma("act", "m", s_m, lambda e, j=j: e.dma_start(Qs[96 + j:97 + j, :, :].bitcast(F32), mh[:, j, :].bitcast(F32)), d)

            def heads(b, hf):
                for pr in range(4):
                    ck = pr % 2
                    cb = bank(6 + ck)
                    for p2 in range(2):
                        for hh in range(2):
                            hl = 2 * pr + hh
                            bk = 1 + hh
                            for y in range(2):
                                kt = 2 * p2 + y
                                t = op("pe", lambda e, bk=bk, y=y, hl=hl, kt=kt: e.matmul(
                                    ps[bk][:, y, :], Ks[0:98, hl, 128 * kt:128 * kt + 128], Qs[0:98, hl, :], start=True, stop=True),
                                    st["stack"], st["md"], t_one, *w_(st["S"][bk - 1]))
                            z = 2 * p2 + hh
                            st["S"][bk - 1] = op("act", lambda e, bk=bk, z=z: e.activation(
                                PT[z][:, :, :], ps[bk][:, :, :], ACT.Exp, scale=SM), t, *w_(st["pt"][z]))
                    for kt in range(4):
                        for hh in range(2):
                            z = 2 * (kt // 2) + hh
                            h = 8 * hf + 2 * pr + hh
                            t = op("pe", lambda e, kt=kt, hh=hh, z=z, h=h, cb=cb: e.matmul(
                                cb[64 * hh:64 * hh + 64, :], V[:, kt, h, :], PT[z][:, kt % 2, :],
                                start=(kt == 0), stop=(kt == 3), skip_group_check=True),
                                st["S"][0], st["S"][1], st["Vr"], *(st["ctx"][ck] or []))
                    for z in range(4):
                        st["pt"][z] = t
                    r = op("dve", lambda e, ck=ck, cb=cb: e.reciprocal(RD[:, ck, :], cb), t)
                    done = []
                    for hh in range(2):
                        h = 8 * hf + 2 * pr + hh
                        done.append(op("dve", lambda e, ck=ck, cb=cb, hh=hh, h=h: e.tensor_tensor(
                            cT[32 * (h % 4):32 * (h % 4) + 32, h // 4, :], cb[64 * hh:64 * hh + 32, :],
                            RD[64 * hh + 32:64 * hh + 64, ck, :], ALU.mult), r, *st["cT"]))
                    st["ctx"][ck] = done
                if hf == 1:
                    st["V"] = [t]
                    st["cT"] = []
                st["cTr"] = done

            def result(b):
                for j in range(4):
                    i = 4 * b + j
                    bk, w = take()
                    for c in range(4):
                        t = op("pe", lambda e, j=j, c=c, bk=bk: e.matmul(bank(bk), cT[:, c, 128 * j:128 * j + 128], wout[:, c, :],
                                                                        start=(c == 0), stop=(c == 3)), *st["cTr"], taw, *w)
                    t_xo[i] = op("dve", lambda e, i=i, bk=bk: e.tensor_tensor(X[:, i, :], X[:, i, :], bank(bk), ALU.add), t, t_xo[i])
                    st["ring01"][bk] = t_xo[i]
                st["cT"] = [t]

            steps = [(b, hf) for b in range(B) for hf in range(2)]
            prepare(0)
            project(0, 0)
            stack()
            for n, (b, hf) in enumerate(steps):
                tm = maxima()
                rows(tm)
                if n + 1 < len(steps):
                    nb, nh = steps[n + 1]
                    if nh == 1:
                        project(nb, 1)
                heads(b, hf)
                if n + 1 < len(steps):
                    nb, nh = steps[n + 1]
                    if nh == 0:
                        prepare(nb)
                        project(nb, 0)
                    stack()
                if hf == 1:
                    result(b)
            return [t_xo[i] for i in range(NT)]

        t_x = ffn(0, t_x)
        phase()
        t_x = attention(t_x)
        phase()
        t_x = ffn(1, t_x)
        s_o = sem("s_o")
        for i in range(NT):
            to = dma("sp", "o", s_o, lambda e, i=i: e.dma_start(o_rows[128 * i:128 * i + 128, :], X[:, i, :]), t_x[i])
        q.wait("sp", to)

        block = ctx.enter_context(nc.Block())
        block.sync(lambda e: q.emit("sp", e))
        block.scalar(lambda e: q.emit("act", e))
        block.vector(lambda e: q.emit("dve", e))
        block.gpsimd(lambda e: q.emit("pool", e))
        block.tensor(lambda e: q.emit("pe", e))


_INS = ["L0_attn_X", "L0_attn_ln_w", "L0_attn_ln_b", "L0_attn_W_in", "L0_attn_W_out", "L0_ffn_gate_w", "L0_ffn_bias",
        "L0_ffn_w_gate", "L0_ffn_w_up", "L0_ffn_w_down", "L0_ffn_ws_gate", "L0_ffn_ws_up", "L0_ffn_ws_down"]


def kernel(**inputs):
    import concourse.bacc as bacc
    from concourse.bass_utils import run_bass_kernel_spmd

    nc = bacc.Bacc("TRN2", target_bir_lowering=False, num_devices=1)
    given = {n: np.ascontiguousarray(inputs[n]) for n in _INS}
    given["consts"], given["rope"] = shape_constants()
    arrays, args = {}, []
    for n, a in given.items():
        arrays["in_" + n] = a
        args.append(nc.dram_tensor("in_" + n, a.shape, mybir.dt.from_np(a.dtype), kind="ExternalInput").ap())
    args.append(nc.dram_tensor("out_0", (B, S, D), F32, kind="ExternalOutput").ap())
    macaron_kernel(nc, *args)
    r = run_bass_kernel_spmd(nc, [arrays], core_ids=[0])
    return r.results[0]["out_0"]
```

```python
from contextlib import ExitStack

import concourse.bass as bass
import numpy as np
from concourse import mybir

F32 = mybir.dt.float32
F32R = mybir.dt.float32r
U32 = mybir.dt.uint32
ALU = mybir.AluOpType
ACT = mybir.ActivationFunctionType
AX = mybir.AxisListType.X

D = 512
T = 2048
NT = 16
B = 4
S = 512
NH = 16
DH = 32
E = 64
K = 6
F = 192
FH = 96
CAP = 96
NG = 8
KG = 4
ROW = D + E
EPS = 1e-5
BIG = 3.0e38
SM = float(1.0 / np.sqrt(np.float32(DH)))

C_ID, C_LM, C_IE, C_TK, C_N = 0, 128, 192, 256, 272


def shape_constants():
    c = np.zeros((128, C_N), np.float32)
    p = np.arange(128)
    c[:, C_ID:C_ID + 128] = np.eye(128)
    g = np.arange(NG)
    c[:, C_LM:C_LM + 64] = (g[None, :] < g[:, None]).astype(np.float32).reshape(1, 64)
    c[:, C_IE:C_IE + 64] = np.arange(E)[None, :]
    c[:, C_TK:C_TK + 16] = T - (np.arange(NT)[None, :] * 128 + p[:, None])
    rot = DH // 2
    inv = (np.float32(1.0) / np.float32(10000.0) ** (np.arange(0, rot, 2, dtype=np.float32) / np.float32(rot))).astype(np.float32)
    ang = np.repeat((np.arange(S, dtype=np.float32)[:, None] * inv[None, :]).astype(np.float32), 2, axis=-1)
    r = np.zeros((DH, 2, S), np.float32)
    r[:, 0, :] = 1.0
    r[:rot, 0, :] = np.cos(ang).T
    r[:rot, 1, :] = np.sin(ang).T * np.where(np.arange(rot) % 2 == 0, -1.0, 1.0)[:, None]
    return c, np.tile(r, (4, 1, 1)).astype(np.float32)


class Queues:

    def __init__(self, nc, ctx):
        self.items = {n: [] for n in ("pe", "act", "dve", "pool", "sp")}
        self.sem = {n: ctx.enter_context(nc.semaphore("done_" + n)) for n in self.items}
        self.count = dict.fromkeys(self.items, 0)
        self.dma_count = {}
        self.dma_last = {}

    def op(self, eng, fn, *waits):
        self.count[eng] += 1
        self.items[eng].append((fn, waits, self.sem[eng], 1))
        return ("done_" + eng, self.sem[eng], self.count[eng])

    def quiet(self, eng, fn, *waits):
        self.items[eng].append((fn, waits, None, 0))

    def dma(self, eng, name, sem, fn, *waits):
        self.dma_count[name] = self.dma_count.get(name, 0) + 16
        self.items[eng].append((fn, waits, sem, 16))
        self.dma_last[name] = (name, sem, self.dma_count[name])
        return self.dma_last[name]

    def wait(self, eng, *waits):
        self.items[eng].append((None, waits, None, 0))

    def all_done(self):
        return [("done_" + n, self.sem[n], v) for n, v in self.count.items() if v] + list(self.dma_last.values())

    def emit(self, eng, e):
        seen = {}
        for fn, waits, sem, by in self.items[eng]:
            for w in waits:
                for name, s, v in (w if isinstance(w, list) else [w]):
                    if seen.get(name, 0) < v:
                        e.wait_ge(s, v)
                        seen[name] = v
            if fn is not None:
                ins = fn(e)
                if sem is not None:
                    ins.then_inc(sem, by)


def macaron_kernel(nc, X_in, ln_w, ln_b, W_in, W_out, gate_w, bias, w_gate, w_up, w_down,
                   ws_gate, ws_up, ws_down, consts, rope, out):
    x_rows = X_in.rearrange("b s d -> (b s) d")
    o_rows = out.rearrange("b s d -> (b s) d")

    with ExitStack() as ctx:
        base = 16 * 1024 + 128
        names = {}

        def at(name, off, shape, dt=F32):
            names[name] = names.get(name, 0) + 1
            return nc.alloc_sbuf_tensor_at(f"{name}_{names[name]}", shape, dt, offset=base + off)

        def sem(name):
            return ctx.enter_context(nc.semaphore(name))

        KB = 1024
        X = at("X", 0, [128, NT, D])
        cst = at("cst", 32 * KB, [128, C_N])
        biasb = at("biasb", 34 * KB + 512, [128, E])
        lnw = at("lnw", 34 * KB + 768, [128, 4])
        lnb = at("lnb", 34 * KB + 800, [128, 4])
        ident = cst[:, C_ID:C_ID + 128]

        ps = [ctx.enter_context(nc.psum_tensor(f"ps{i}", [128, 2, 512], F32)) for i in range(4)]

        def bank(i):
            return ps[i // 2][:, i % 2, :]

        q = Queues(nc, ctx)
        op, dma = q.op, q.dma

        s_x = [sem(f"s_x{g}") for g in range(4)]
        s_c = sem("s_c")
        s_ln = sem("s_ln")
        s_fw = sem("s_fw")
        s_gw = sem("s_gw")
        s_aw = sem("s_aw")
        AW = 156 * KB
        win = at("win", AW, [128, 4, 3 * D])
        wout = at("wout", AW + 24 * KB, [128, 4, D])
        rp = at("rp", AW + 32 * KB, [128, 2, S])

        tx = [dma("sp", f"x{g}", s_x[g], lambda e, g=g: e.dma_start(
            X[:, 4 * g:4 * g + 4, :], x_rows[512 * g:512 * g + 512, :].rearrange("(i p) d -> p i d", p=128)))
            for g in range(4)]
        tc = dma("act", "c", s_c, lambda e: e.dma_start(cst[:, :], consts))
        tc = dma("act", "c", s_c, lambda e: e.dma_start(biasb[:, :], bias.partition_broadcast(128)))
        tln = dma("act", "ln", s_ln, lambda e: e.dma_start(lnw[:, :], ln_w.rearrange("(p c) -> p c", c=4)))
        tln = dma("act", "ln", s_ln, lambda e: e.dma_start(lnb[:, :], ln_b.rearrange("(p c) -> p c", c=4)))

        t_x = [tx[i // 4] for i in range(NT)]

        free = [None, None]
        turn = [0]

        def take():
            turn[0] += 1
            j = turn[0] % 2
            return j, ([free[j]] if free[j] else [])

        def rstd(src_var, ve, sq, r, t, wait):
            a = op("dve", lambda e: e.tensor_scalar(ve, src_var, EPS, None, ALU.add), wait)
            b = op("act", lambda e: e.activation(sq, ve, ACT.Sqrt), a)
            c = op("dve", lambda e: e.reciprocal(r, sq), b)
            c = op("dve", lambda e: e.tensor_tensor(t, r, r, ALU.mult), c)
            c = op("dve", lambda e: e.tensor_tensor(t, t, ve, ALU.mult), c)
            c = op("dve", lambda e: e.tensor_scalar(t, t, -0.5, 1.5, ALU.mult, ALU.add), c)
            return op("dve", lambda e: e.tensor_tensor(r, r, t, ALU.mult), c)

        def ffn(n, y, ring_at, gw_at, ws_at, A1, A2, t_x):
            NR, NB = 7, 6
            ring = [(at("gu", r * KB, [128, 4, 2, F]), at("wd", (r + 6) * KB, [FH, 2, D])) for r in ring_at]
            gw = at("gw", gw_at * KB, [128, 4, E])
            wsgu = at("wsgu", ws_at * KB, [128, 4, 2, F])
            wsd = at("wsd", (ws_at + 6) * KB, [128, 2, D])
            A1, A2 = A1 * KB, A2 * KB
            xnT = at("xnT", A1, [128, 4, T])
            XN = at("XN", A1 + 32 * KB, [128, 4, D])
            buf = [at("buf", A1 + j * 2304, [CAP, ROW]) for j in range(NB)]
            o = A1 + NB * 2304
            bufT = [at("bufT", o + j * 1536, [128, 4, CAP]) for j in range(2)]
            sg = [at("sg", o + 3072 + j * 768, [FH, 2, CAP]) for j in range(2)]
            hH = [at("hH", o + 4608 + j * 768, [FH, 2, CAP], F32R) for j in range(2)]
            hL = [at("hL", o + 12288 + j * 768, [FH, 2, CAP], F32R) for j in range(2)]
            hF = [at("hF", o + 13824 + j * 768, [FH, 2, CAP]) for j in range(2)]
            osb = [at("osb", o + 6144 + j * 2048, [CAP, D]) for j in range(3)]
            R = [at(f"R{j}", A2 + 4 * KB * j, [128, NT, E]) for j in range(7)]
            wdH = [at("wdH", v, [FH, 2, D], F32R) for v in (A1 + 32 * KB, A2 + 36 * KB)]
            wdL = [at("wdL", v, [FH, 2, D], F32R) for v in (A1 + 36 * KB, A2 + 40 * KB)]
            keyT = at("keyT", A2 + 32 * KB, [128, T // 2])
            sgs = at("sgs", A2 + 36 * KB, [FH, 2, S])
            hTs = [at("hTs", A2 + 40 * KB, [FH, 2, S]), at("hTs", A2 + 4 * KB, [FH, 2, S])]
            A3 = A2 + 44 * KB
            A4 = 207 * KB - 256
            BS = at("BS", A4, [128, NT, 6])
            MV = at("MV", A4 + 384, [128, NT, 2])
            VE, SQ, RS, TM = [at("sm", A4 + 512 + 64 * j, [128, NT]) for j in range(4)]
            V8 = at("V8", A3 + 768, [128, NT, 8])
            I8 = at("I8", A3 + 1280, [128, NT, 8], U32)
            i6 = at("i6", A3 + 2304, [128, NT])
            den = at("den", A3 + 2368, [128, NT])
            lst = at("lst", A3 + 2432, [128, CAP])
            cand = at("cand", A3 + 2816, [E, 2 * CAP])
            first = at("first", A3 + 3584, [E, CAP])
            tok = at("tok", A3 + 3968, [CAP, E], U32)
            tokf = at("tokf", A3 + 4224, [CAP, E])
            assert A3 + 4480 <= A4

            xn_d = nc.dram_tensor(f"xn_d{n}", [T, ROW], F32, kind="Internal").ap()
            s_ring = [sem(f"s_ring{n}_{r}") for r in range(NR)]
            s_xn = [sem(f"s_xn{n}_{r}") for r in range(4)]
            s_w = sem(f"s_w{n}")
            s_buf = [sem(f"s_buf{n}_{r}") for r in range(NB)]
            s_out = sem(f"s_out{n}")
            s_y = sem(f"s_y{n}")

            def load(x, *waits):
                gu, wd = ring[x % NR]
                nm, s = f"ring{n}_{x % NR}", s_ring[x % NR]
                dma("sp", nm, s, lambda e: e.dma_start(gu[:, :, 0, :], w_gate[x].rearrange("(p c) f -> p c f", c=4)), *waits)
                dma("sp", nm, s, lambda e: e.dma_start(gu[:, :, 1, :], w_up[x].rearrange("(p c) f -> p c f", c=4)))
                return dma("sp", nm, s, lambda e: e.dma_start(wd[:, :, :], w_down[x].rearrange("(c p) h -> p c h", c=2)))

            tgw, tfw = [], []

            def load_router(*waits):
                tgw.append(dma("sp", "gw", s_gw, lambda e: e.dma_start(gw[:, :, :], gate_w.rearrange("(p c) n -> p c n", c=4)), *waits))

            def load_shared(*waits):
                dma("sp", "fw", s_fw, lambda e: e.dma_start(wsgu[:, :, 0, :], ws_gate.rearrange("(p c) n -> p c n", c=4)), *waits)
                dma("sp", "fw", s_fw, lambda e: e.dma_start(wsgu[:, :, 1, :], ws_up.rearrange("(p c) n -> p c n", c=4)))
                tfw.append(dma("sp", "fw", s_fw, lambda e: e.dma_start(wsd[0:FH, :, :], ws_down.rearrange("(c p) n -> p c n", c=2))))

            tr, tt, t_evT, t_lg, t_xnd, t_ring = {}, {}, {}, {}, {}, {}

            def moments(i):
                t = op("dve", lambda e: e.bn_stats(BS[:, i, :], X[:, i, :]), t_x[i])
                tr[i] = op("dve", lambda e: e.bn_aggr(MV[:, i, :], BS[:, i, :]), t)

            def roots(lo, hi):
                gs = slice(lo, hi)
                t = rstd(MV[:, gs, 1], VE[:, gs], SQ[:, gs], RS[:, gs], TM[:, gs], tr[hi - 1])
                for i in range(lo, hi):
                    tr[i] = t

            def tile(i, *waits):
                w = [t_evT[i - 4], t_xnd[i - 4]] if i >= 4 else []
                tn = op("dve", lambda e: e.tensor_scalar(XN[:, i % 4, :], X[:, i, :], MV[:, i, 0:1], RS[:, i:i + 1],
                                                         ALU.subtract, ALU.mult), tr[i], *w)
                t_xnd[i] = dma("sp", f"xn{n}_{i % 4}", s_xn[i % 4], lambda e: e.dma_start(
                    xn_d[128 * i:128 * i + 128, 0:D], XN[:, i % 4, :]), tn)
                bk, w = take()
                for c in range(4):
                    tt[i] = op("pe", lambda e, c=c: e.transpose(bank(bk)[:, 128 * c:128 * c + 128], XN[:, i % 4, c:D:4], ident),
                               tn, tc, *w)
                free[bk] = t_evT[i] = op("act", lambda e: e.copy(xnT[:, :, 128 * i:128 * i + 128],
                                                                 bank(bk).rearrange("p (c t) -> p c t", c=4)), tt[i], *waits)

            def logits(i):
                for c in range(4):
                    t_lg[i] = op("pe", lambda e, c=c: e.matmul(
                        bank(4 + i // 8)[:, 64 * (i % 8):64 * (i % 8) + 64],
                        xnT[:, c, 128 * i:128 * i + 128], gw[:, c, :], start=(c == 0), stop=(c == 3)), t_evT[i], tgw)

            def load_ring(*waits):
                for x in range(NR):
                    t_ring[x] = load(x, *waits)

            t_hs, t_up = {}, {}

            def shared_up(gq, js=range(4), *waits):
                w = [t_hs[gq - 1]] if gq else []
                for j in js:
                    for c in range(4):
                        t_up[gq] = op("pe", lambda e, j=j, c=c: e.matmul(
                            bank(2 + j if j < 2 else 4 + j)[0:FH, :], wsgu[:, c, j // 2, FH * (j % 2):FH * (j % 2) + FH],
                            xnT[:, c, S * gq:S * gq + S], start=(c == 0), stop=(c == 3)), tfw, t_evT[4 * gq + 3], *w, *waits)

            def rest():
                t_sh, t_dn, t_shc, w_out = {}, {}, {}, []

                t_si = {}

                def shared_silu(gq):
                    w = [t_hs[gq - 1]] if gq else []
                    t_si[gq] = op("act", lambda e: e.activation(sgs[:, :, :], ps[1][0:FH, :, :], ACT.Silu), t_up[gq], *w)

                def shared_mul(gq, *waits):
                    w = [t_dn[gq - 2]] if gq >= 2 else []
                    t_hs[gq] = op("dve", lambda e: e.tensor_tensor(hTs[gq % 2][:, :, :], sgs[:, :, :], ps[3][0:FH, :, :], ALU.mult), t_si[gq], *w, *waits)

                def shared_down(gq):
                    for j in range(4):
                        i = 4 * gq + j
                        w = [t_shc[i - 2]] if i >= 2 else [t_evT[NT - 1]]
                        for h in range(2):
                            t_dn[gq] = op("pe", lambda e, j=j, i=i, h=h: e.matmul(
                                bank(i % 2), hTs[gq % 2][:, h, 128 * j:128 * j + 128], wsd[0:FH, h, :],
                                start=(h == 0), stop=(h == 1)), t_hs[gq], *w)
                        w = [t_sh[i - 4]] if i >= 4 else [t_xnd[NT - 4 + i]]
                        t_shc[i] = op("act", lambda e, i=i: e.activation(XN[:, i % 4, :], bank(i % 2), ACT.Copy, scale=0.5), t_dn[gq], *w)
                        t_sh[i] = op("pool", lambda e, i=i: e.tensor_tensor(X[:, i, :], X[:, i, :], XN[:, i % 4, :], ALU.add), t_shc[i])
                        w_out.append(dma("act", f"y{n}", s_y, lambda e, i=i: e.dma_start(y[128 * i:128 * i + 128, :], X[:, i, :]), t_sh[i]))

                SC, SB, P1, P2, SEL, W, P3 = [r[:, :, :] for r in R]
                flat = lambda ap: ap.rearrange("p i e -> p (i e)")
                grp = lambda ap: ap.rearrange("p i (g j) -> p (i g) j", j=8)
                bE = lambda ap: ap.unsqueeze(2).to_broadcast([128, NT, E])
                cE = lambda o: cst[:, o:o + 64].unsqueeze(1).to_broadcast([128, NT, E])
                dv = lambda fn, *w: op("dve", fn, *w)
                TT = lambda o, a, b, f: (lambda e: e.tensor_tensor(o, a, b, f))

                t_sc = op("act", lambda e: e.activation(SC.rearrange("p (a i) e -> p a (i e)", a=2), ps[2][:, :, :], ACT.Sigmoid), t_lg[NT - 1])
                ahead = n

                def shared_step(k, *waits):
                    if k < 4:
                        shared_mul(k, *waits)
                    if k + 1 < 4:
                        shared_up(k + 1)
                        shared_silu(k + 1)

                shared_silu(0)
                if ahead:
                    shared_step(0)
                t = dv(TT(SB, SC, biasb[:, :].unsqueeze(1).to_broadcast([128, NT, E]), ALU.add), t_sc, tc)
                s8 = grp(SB)
                part = lambda ap, o, m, j: flat(ap)[:, o:o + m * j].rearrange("p (m j) -> p m j", j=j)
                h1, l1 = part(P1, 0, 128, 4), part(P1, 512, 128, 4)
                h2, l2, u2 = part(P2, 0, 128, 2), part(P2, 256, 128, 2), part(P2, 512, 128, 2)
                h3, l3, u3, gsum, rank, msk, neg = (flat(P3)[:, 128 * j:128 * j + 128] for j in range(7))
                dv(TT(h1, s8[:, :, 0::2], s8[:, :, 1::2], ALU.max), t)
                t = dv(TT(l1, s8[:, :, 0::2], s8[:, :, 1::2], ALU.min), t)
                dv(TT(h2, h1[:, :, 0::2], h1[:, :, 1::2], ALU.max), t)
                dv(TT(l2, h1[:, :, 0::2], h1[:, :, 1::2], ALU.min), t)
                t = dv(TT(u2, l1[:, :, 0::2], l1[:, :, 1::2], ALU.max), t)
                t = dv(TT(l2, l2, u2, ALU.max), t)
                dv(TT(h3, h2[:, :, 0], h2[:, :, 1], ALU.max), t)
                dv(TT(l3, h2[:, :, 0], h2[:, :, 1], ALU.min), t)
                t = dv(TT(u3, l2[:, :, 0], l2[:, :, 1], ALU.max), t)
                t = dv(TT(l3, l3, u3, ALU.max), t)
                t = dv(TT(gsum, h3, l3, ALU.add), t)
                G3 = gsum.rearrange("p (i g) -> p i g", g=NG)
                ga = G3.unsqueeze(2).to_broadcast([128, NT, NG, NG])
                gb = G3.unsqueeze(3).to_broadcast([128, NT, NG, NG])
                r4 = lambda ap: ap.rearrange("p i (g j) -> p i g j", j=NG)
                dv(TT(r4(P1), ga, gb, ALU.is_gt), t)
                t = dv(TT(r4(P2), ga, gb, ALU.is_equal), t)
                t = dv(TT(P2, P2, cE(C_LM), ALU.mult), t)
                t = dv(TT(P1, P1, P2, ALU.add), t)
                t = dv(lambda e: e.tensor_reduce(rank, grp(P1), AX, ALU.add), t)
                t = dv(lambda e: e.tensor_scalar(msk, rank, float(KG), None, ALU.is_lt), t)
                t = dv(lambda e: e.tensor_scalar(neg, msk, BIG, -BIG, ALU.mult, ALU.add), t)
                bg = lambda ap: ap.unsqueeze(2).to_broadcast([128, 128, 8])
                t = dv(TT(grp(P1), s8, bg(neg), ALU.add), t)
                shared_step(ahead, t)
                for i in range(NT):
                    tv = dv(lambda e, i=i: e.max(V8[:, i, :], P1[:, i, :]), t)
                tk = cst[:, C_TK:C_TK + 16].unsqueeze(2).to_broadcast([128, NT, E])
                a = dv(TT(P3, P1, bE(V8[:, :, K - 1]), ALU.is_gt), tv)
                a2 = op("pool", lambda e: e.tensor_scalar(W, P3, float(T), None, ALU.mult), a)
                g = op("pool", TT(W, W, tk, ALU.add), a2)
                for i in range(NT):
                    ti = dv(lambda e, i=i: e.max_index(I8[:, i, :], V8[:, i, :], P1[:, i, :]), tv)
                t = dv(lambda e: e.tensor_copy(i6[:, :], I8[:, :, K - 1]), ti)
                dv(TT(SEL, P1, bE(V8[:, :, K - 1]), ALU.is_equal), tv)
                t = dv(TT(P2, cE(C_IE), bE(i6[:, :]), ALU.is_le), t)
                t_eq = dv(TT(P2, P2, SEL, ALU.mult), t)
                t_key = dv(lambda e: e.scalar_tensor_tensor(out=P1, in0=P2, scalar=float(T), in1=W, op0=ALU.mult, op1=ALU.add), t_eq, g)
                for i in range(8):
                    tp = op("pe", lambda e, i=i: e.transpose(bank(4 + i // 4)[:, 128 * (i % 4):128 * (i % 4) + 128],
                                                             flat(P1)[:, 128 * i:128 * i + 128], ident), t_key, t_sc)
                shared_down(0)
                t = op("pool", TT(SEL, P2, P3, ALU.add), t_eq, a)
                t_sel = op("pool", TT(P2, SC, SEL, ALU.mult), t)

                def weights():
                    t = dv(lambda e: e.tensor_reduce(den[:, :], P2, AX, ALU.add), t_sel)
                    t = dv(lambda e: e.reciprocal(den[:, :], den[:, :]), t)
                    t = dv(lambda e: e.tensor_scalar(den[:, :], den[:, :], 1.25, None, ALU.mult), t)
                    t = op("pool", TT(W, P2, bE(den[:, :]), ALU.mult), t)
                    return dma("act", f"w{n}", s_w, lambda e: e.dma_start(xn_d[:, D:ROW].rearrange("(i p) e -> p i e", p=128), W), t)

                if not ahead:
                    shared_step(1)
                    shared_down(1)
                t, src = tp, ps[2][:, :, :].rearrange("p a b -> p (a b)")
                for r in range(CAP // 8):
                    t = dv(lambda e, r=r, src=src: e.max(lst[:, 8 * r:8 * r + 8], src), t)
                    if r < CAP // 8 - 1:
                        t = t_kT = dv(lambda e, r=r, src=src: e.match_replace(keyT[:, :], lst[:, 8 * r:8 * r + 8], src, 0.0), t)
                    src = keyT[:, :]
                    if r == 5:
                        t_wd = weights()
                    if r == 2 and ahead:
                        shared_step(2)
                        shared_down(1)
                    if r == 6 and not ahead:
                        shared_step(2)
                    if r == 11 and ahead:
                        shared_step(3)
                        shared_down(2)
                dv(lambda e: e.tensor_copy(cand[:, 0:CAP], lst[0:E, :]), t)
                t = dv(lambda e: e.tensor_copy(cand[:, CAP:2 * CAP], lst[E:128, :]), t)
                for r in range(CAP // 8):
                    t = dv(lambda e, r=r: e.max(first[:, 8 * r:8 * r + 8], cand[:, :]), t)
                    if r < CAP // 8 - 1:
                        t = dv(lambda e, r=r: e.match_replace(cand[:, :], first[:, 8 * r:8 * r + 8], cand[:, :], 0.0), t)
                tp = op("pe", lambda e: e.transpose(bank(4)[0:CAP, 0:E], first[:, :], cst[0:E, C_ID:C_ID + E]), t, t_kT)
                t = dv(lambda e: e.tensor_scalar(tokf[:, :], bank(4)[0:CAP, 0:E], float(T), float(T), ALU.is_gt, ALU.mult), tp)
                t_tok = dv(lambda e: e.scalar_tensor_tensor(out=tok[:, :], in0=tokf[:, :], scalar=float(T), in1=bank(4)[0:CAP, 0:E],
                                                            op0=ALU.add, op1=ALU.subtract), t)
                if not ahead:
                    shared_step(3)

                t_buf, t_bT, t_gu, t_h, t_wL, t_d, t_ev, t_out = {}, {}, {}, {}, {}, {}, {}, {}

                def gather(x):
                    w = [t_ev[x - NB]] if x >= NB else [t_tok, t_wd, t_up[3]] + [t_xnd[i] for i in range(NT - 4, NT)]
                    t_buf[x] = dma("pool", f"buf{n}_{x % NB}", s_buf[x % NB], lambda e: e.indirect_dma_start(
                        out=buf[x % NB][:, :], out_offset=None, in_=xn_d, in_offset=bass.IndirectOffsetOnAxis(ap=tok[:, x:x + 1], axis=0),
                        bounds_check=T - 1, oob_is_err=True), *w)

                for x in range(NB):
                    gather(x)
                if not ahead:
                    shared_down(2)
                shared_down(3)
                for st in range(E + 2):
                    x = st
                    if x < E:
                        w = [t_bT[x - 2]] if x >= 2 else [t_shc[NT - 1]]
                        for c in range(4):
                            tt = op("pe", lambda e, x=x, c=c: e.transpose(bank(x % 2)[:, CAP * c:CAP * c + CAP],
                                                                          buf[x % NB][:, c:D:4], cst[0:CAP, C_ID:C_ID + CAP]), t_buf[x], *w)
                        w = [t_gu[x - 2]] if x >= 2 else []
                        t_bT[x] = op("act", lambda e, x=x: e.copy(bufT[x % 2][:, :, :], bank(x % 2)[:, 0:4 * CAP].rearrange("p (c t) -> p c t", c=4)), tt, *w)
                    x = st - 1
                    if 0 <= x < E:
                        gu, wd = ring[x % NR]
                        w = [t_h[x - 2]] if x >= 2 else [t_hs[3]]
                        for j in range(4):
                            for c in range(4):
                                t_gu[x] = op("pe", lambda e, x=x, gu=gu, j=j, c=c: e.matmul(
                                    bank(2 + x % 2)[0:FH, CAP * j:CAP * j + CAP], gu[:, c, j // 2, FH * (j % 2):FH * (j % 2) + FH],
                                    bufT[x % 2][:, c, :], start=(c == 0), stop=(c == 3)), t_bT[x], t_ring[x], *w)
                        w = [t_h[x - 2]] if x >= 2 else []
                        a = op("act", lambda e, x=x: e.activation(sg[x % 2][:, :, :].rearrange("p a b -> p (a b)"),
                                                                  bank(2 + x % 2)[0:FH, 0:2 * CAP], ACT.Silu), t_gu[x], *w)
                        fl = lambda v: v.rearrange("p a b -> p (a b)")
                        w = [t_d[x - 2]] if x >= 2 else []
                        m = op("dve", lambda e, x=x: e.tensor_tensor(fl(hF[x % 2][:, :, :]), fl(sg[x % 2][:, :, :]),
                                                                     bank(2 + x % 2)[0:FH, 2 * CAP:4 * CAP], ALU.mult), a, *w)
                        a = op("act", lambda e, x=x: e.copy(hH[x % 2][:, :, :], hF[x % 2][:, :, :]), m, *w)
                        w += [t_sh[NT - 1], t_dn[3], t_ring[x]]
                        b = op("act", lambda e, x=x, wd=wd: e.copy(wdH[x % 2][:, :, :], wd[:, :, :]), *w)
                        t_wL[x] = op("dve", lambda e, x=x, wd=wd: e.tensor_tensor(wdL[x % 2][:, :, :], wd[:, :, :], wdH[x % 2][:, :, :].bitcast(F32), ALU.subtract), b)
                        t_h[x] = op("dve", lambda e, x=x: e.tensor_tensor(hL[x % 2][:, :, :], hF[x % 2][:, :, :], hH[x % 2][:, :, :].bitcast(F32), ALU.subtract), a)
                    x = st - 2
                    if 0 <= x < E:
                        w = [t_ev[x - 2]] if x >= 2 else [t_tok]
                        hw = [(hH, wdH), (hH, wdL), (hL, wdH)]
                        for h in range(2):
                            for k, (u, v) in enumerate(hw):
                                t_d[x] = op("pe", lambda e, x=x, h=h, k=k, u=u, v=v: e.matmul(
                                    bank(4 + x % 2)[0:CAP, :], u[x % 2][:, h, :], v[x % 2][:, h, :],
                                    start=(h == 0 and k == 0), stop=(h == 1 and k == 2)), t_h[x], t_wL[x], *w)
                        w = [t_out[x - 3]] if x >= 3 else []
                        t_ev[x] = op("dve", lambda e, x=x: e.tensor_scalar(osb[x % 3][:, :], bank(4 + x % 2)[0:CAP, :],
                                                                           buf[x % NB][:, D + x:D + x + 1], None, ALU.mult), t_d[x], *w)
                        if x + NB < E:
                            gather(x + NB)
                        t_out[x] = dma("pool", f"out{n}", s_out, lambda e, x=x: e.indirect_dma_start(
                            out=y, out_offset=bass.IndirectOffsetOnAxis(ap=tok[:, x:x + 1], axis=0), in_=osb[x % 3][:, :], in_offset=None,
                            bounds_check=T - 1, oob_is_err=True, compute_op=ALU.add), t_ev[x], *(w_out[-1:] if x == 0 else [t_out[x - 1]]))
                        if x + NR < E:
                            t_ring[x + NR] = load(x + NR, t_d[x])
                        elif n == 0:
                            attention_weights(x + NR - E, t_d[x], t_tok, t_wd)

                return t_out[E - 1]

            return dict(load_router=load_router, load_shared=load_shared, load_ring=load_ring, moments=moments, roots=roots,
                        tile=tile, logits=logits, shared_up=shared_up, rest=rest)

        taw = []

        def attention_weights(k, *waits):
            if k < 4:
                parts = [(win[:, k, :], W_in.rearrange("(p c) n -> p c n", c=4)[:, k, :])]
            elif k == 4:
                parts = [(rp[:, :, :], rope)]
            elif k == 5:
                parts = [(wout[:, :, :], W_out.rearrange("(c p) n -> p c n", c=4))]
            else:
                parts = []
            for d, v in parts:
                taw[:] = [dma("sp", "aw", s_aw, lambda e: e.dma_start(d, v), *waits)]

        def phase():
            done = q.all_done()
            for n in q.items:
                q.wait(n, done)

        def attention(t_x, taw, f2, t_x2):
            AT = 35 * KB
            St = [at("St", AT + 16 * KB * j, [98, 2, 4, S], F32R) for j in range(3)]
            xT = [at("xT", AT + 48 * KB + 8 * KB * j, [128, 4, S]) for j in range(2)]
            V = [at("V", AT + 64 * KB + 8 * KB * j, [128, 4, D]) for j in range(2)]
            NP = 12
            PT = [at("PT", AT + 80 * KB + 2 * KB * j, [128, S]) for j in range(NP)]
            HI = at("HI", AT + 104 * KB, [128, 2, S], F32R)
            LO = at("LO", AT + 108 * KB, [128, 2, S])
            cT = at("cT", AT + 112 * KB, [128, 4, S])
            o = AW + 36 * KB
            mh = at("mh", o, [4, 2, S], F32R)
            t2 = at("t2", o + 4 * KB, [128, 2, S])
            ZH = [at("ZH", o + 8 * KB + 2 * KB * j, [128, D]) for j in range(2)]
            RD = at("RD", o + 12 * KB, [128, S])
            o += 14 * KB
            on = at("on", o, [128, 32])
            Mx = at("Mx", o + 128, [128, 4, 4])
            BS = at("BS", o + 192, [128, 4, 6])
            MV = at("MV", o + 288, [128, 4, 2])
            VE, SQ, RS, TM, R2, OP, NM = [at("sm", o + 320 + 32 * j, [128, 4])[:, :] for j in range(7)]
            s_st = [[sem(f"s_st{j}_{h}") for h in range(4)] for j in range(3)]
            s_m = [sem(f"s_m{j}") for j in range(3)]
            NU = 4 * B

            t_on = op("dve", lambda e: e.memset(on[:, :], 1.0))
            for j in range(3):
                t_st1 = op("pool", lambda e, j=j: e.memset(St[j][96:98, 1, :, :].bitcast(F32), 1.0))
            q.wait("pool", t_st1)

            t_stat, t_xT, t_V, t_hl, t_st, t_max, t_md, t_rows = {}, {}, {}, {}, {}, {}, {}, {}
            t_zh, t_xz, t_P, t_ST, t_exp, t_pv, t_nrm, t_O, t_xo, t_Vmm = {}, {}, {}, {}, {}, {}, {}, {}, {}, {}
            got = lambda d, k: [d[k]] if k in d else []

            def stats(b):
                for j in range(4):
                    t = op("dve", lambda e, j=j: e.bn_stats(BS[:, j, :], X[:, 4 * b + j, :]), t_x[4 * b + j])
                for j in range(4):
                    t = op("dve", lambda e, j=j: e.bn_aggr(MV[:, j, :], BS[:, j, :]), t, *got(t_xz, 4 * b - 1))
                t = rstd(MV[:, :, 1], VE, SQ, RS, TM, t)
                t = op("dve", lambda e: e.tensor_tensor(R2, RS, RS, ALU.mult), t)
                t = op("dve", lambda e: e.tensor_tensor(R2, R2, MV[:, :, 1], ALU.mult), t)
                op("dve", lambda e: e.tensor_scalar(OP, RS, 1.0, None, ALU.add), t)
                t3 = op("dve", lambda e: e.scalar_tensor_tensor(out=NM, in0=MV[:, :, 0], scalar=-1.0, in1=RS, op0=ALU.mult, op1=ALU.mult), t)
                u = rstd(R2, VE, SQ, R2, TM, t3)
                t_stat[b] = op("dve", lambda e: e.tensor_tensor(R2, R2, RS, ALU.mult), u)

            def center(i):
                j = i % 4
                z = ZH[i % 2]
                t_zh[i] = op("dve", lambda e: e.tensor_scalar(z[:, :], X[:, i, :], MV[:, j, 0:1], R2[:, j:j + 1], ALU.subtract, ALU.mult),
                             t_stat[i // 4], *got(t_xT, i - 2))
                t_xz[i] = op("pool", lambda e: e.tensor_scalar(X[:, i, :], X[:, i, :], OP[:, j:j + 1], NM[:, j:j + 1], ALU.mult, ALU.add), t_zh[i])

            def tile(i):
                b, j = i // 4, i % 4
                z = ZH[i % 2]
                bk, w = take()
                for c in range(4):
                    t = op("pe", lambda e, c=c: e.transpose(bank(bk)[:, 128 * c:128 * c + 128], z[:, c:D:4], ident), t_zh[i], *w)
                for c in range(4):
                    t_xT[i] = op("act", lambda e, c=c: e.activation(
                        xT[b % 2][:, c, 128 * j:128 * j + 128], bank(bk)[:, 128 * c:128 * c + 128], ACT.Identity,
                        bias=lnb[:, c:c + 1], scale=lnw[:, c:c + 1]), t, tln, *got(t_P, 4 * b - 5), *got(t_Vmm, 4 * b - 5))
                free[bk] = t_xT[i]

            held, t_dr, t_mh = {}, {}, {}

            def value(i, half):
                b, j = i // 4, i % 4
                if half == 0:
                    held["V"] = take()
                bk, w = held["V"]
                for c in (2 * half, 2 * half + 1):
                    t_Vmm[i] = op("pe", lambda e, c=c: e.matmul(bank(bk), xT[b % 2][:, c, 128 * j:128 * j + 128], win[:, c, 2 * D:3 * D],
                                                                start=(c == 0), stop=(c == 3)), t_xT[i], taw, *w)
                if half:
                    t_V[i] = op("act", lambda e: e.copy(V[b % 2][:, j, :], bank(bk)), t_Vmm[i], *got(t_pv, (4 * b - 5, 3)))
                    free[bk] = t_V[i]

            def project(u, k, half):
                b, g = u // 4, u % 4
                col = D * k + 128 * g
                if half == 0:
                    held["P"] = take()
                bk, w = held["P"]
                for c in (2 * half, 2 * half + 1):
                    t_P[u] = op("pe", lambda e, c=c: e.matmul(bank(bk), win[:, c, col:col + 128], xT[b % 2][:, c, :],
                                                              start=(c == 0), stop=(c == 3)), t_xT[4 * b + 3], taw, *w)
                if not half:
                    return
                w = got(t_st, u - 1)
                a = op("dve", lambda e: e.stream_shuffle(t2[:, k, :], bank(bk), [i ^ 1 for i in range(32)]), t_P[u], *got(t_hl, (u - 1, k)))
                a = op("pool", lambda e: e.tensor_tensor(t2[:, k, :], t2[:, k, :], rp[:, 1, :], ALU.mult), a, taw)
                free[bk] = d = op("dve", lambda e: e.tensor_tensor(LO[:, k, :], bank(bk), rp[:, 0, :], ALU.mult), t_P[u], taw, *w)
                t_hl[u, k] = op("pool", lambda e: e.tensor_tensor(LO[:, k, :], LO[:, k, :], t2[:, k, :], ALU.add), d, a)

            def split(u, k):
                h = op("act", lambda e: e.copy(HI[:, k, :], LO[:, k, :]), t_hl[u, k], *got(t_st, u - 1))
                t_hl[u] = op("pool", lambda e: e.tensor_tensor(LO[:, k, :].bitcast(F32R), LO[:, k, :], HI[:, k, :].bitcast(F32), ALU.subtract), h)

            def stack(u):
                d = St[u % 3]
                w = got(t_ST, u - 3)
                q_, k_ = slice(0, 1), slice(1, 2)
                t_st[u] = []
                for j in range(4):
                    for s_, src, x in ((0, HI, slice(0, 2)), (1, HI, q_), (1, LO, k_), (2, LO, q_), (2, HI, k_)):
                        v = src[32 * j:32 * j + 32, x, :]
                        v = v.bitcast(F32) if src is HI else v
                        t = dma("sp", f"st{u % 3}_{j}", s_st[u % 3][j], lambda e, j=j, s_=s_, v=v, x=x: e.dma_start(
                            d[32 * s_:32 * s_ + 32, x, j, :].bitcast(F32), v), t_hl[u], *w)
                    t_st[u].append(t)

            def scores(u, j):
                d, hl, qt = St[u % 3], j // 4, j % 4
                n = 16 * u + j
                bk = 4 + j % 2
                t = op("pe", lambda e: e.matmul(bank(bk), d[0:96, 0, hl, 128 * qt:128 * qt + 128], d[0:96, 1, hl, :],
                                                start=True, stop=True), t_st[u][hl], *got(t_max, n - 2))
                t_max[n] = op("dve", lambda e: e.tensor_reduce(Mx[:, qt, hl:hl + 1], bank(bk), AX, ALU.max, negate=True), t, *got(t_rows, u - 1))

            def rows(u):
                bk, w = take()
                for qt in range(4):
                    t_rows[u] = op("pe", lambda e, qt=qt: e.transpose(bank(bk)[0:4, 128 * qt:128 * qt + 128], Mx[:, qt, :], ident),
                                   t_max[16 * u + 15], *w)
                a = op("act", lambda e: e.copy(mh[:, 0, :], bank(bk)[0:4, :]), t_rows[u], *got(t_md, u - 1))
                free[bk] = t_mh[u] = op("dve", lambda e: e.tensor_tensor(mh[:, 1, :], bank(bk)[0:4, :], mh[:, 0, :].bitcast(F32), ALU.subtract), a)

            def fill(u):
                for j in range(2):
                    t_md[u] = dma("act", f"m{u % 3}", s_m[u % 3], lambda e, j=j: e.dma_start(
                        St[u % 3][96 + j:97 + j, 0, :, :].bitcast(F32), mh[:, j, :].bitcast(F32)), t_mh[u], *got(t_ST, u - 3))

            def expo(u, j):
                d, hl, kt = St[u % 3], j % 4, j // 4
                n = 16 * u + j
                bk = 2 + j % 2
                t_ST[u] = op("pe", lambda e: e.matmul(bank(bk), d[0:98, 1, hl, 128 * kt:128 * kt + 128], d[0:98, 0, hl, :],
                                                      start=True, stop=True), t_st[u], t_md[u], t_st1, *got(t_exp, n - 2))
                m = n - NP
                t_exp[n] = op("act", lambda e: e.activation(PT[n % NP][:, :], bank(bk), ACT.Exp, scale=SM), t_ST[u],
                              *(got(t_pv, (m // 16, m % 16 // 4)) if m >= 0 else []))

            def weigh(u, kt, what):
                b = u // 4
                for hl in range(4):
                    n = 16 * u + 4 * kt + hl
                    h = 4 * (u % 4) + hl
                    lhs = V[b % 2][:, kt, DH * h:DH * h + DH] if what == 0 else on[:, :]
                    t_pv[u, kt] = op("pe", lambda e, hl=hl, lhs=lhs, n=n: e.matmul(
                        ps[3][32 * hl:32 * hl + 32, what, :], lhs, PT[n % NP][:, :], start=(kt == 0), stop=(kt == 3),
                        tile_position=(0, 32 * hl), skip_group_check=True),
                        t_exp[n], t_V[4 * b + kt], t_on, *got(t_dr, u - 1))

            def drain(u):
                op("act", lambda e: e.copy(RD[:, :], ps[3][:, 1, :]), t_pv[u, 3], *got(t_nrm, u - 1))
                t_dr[u] = op("act", lambda e: e.copy(cT[:, u % 4, :], ps[3][:, 0, :]), t_pv[u, 3], *got(t_O, u // 4 - 1))

            def norm(u, k):
                c = slice(128 * k, 128 * k + 128)
                r = op("dve", lambda e: e.reciprocal(RD[:, c], RD[:, c]), t_dr[u])
                if k == 3:
                    t_nrm[u] = op("pool", lambda e: e.tensor_tensor(cT[:, u % 4, :], cT[:, u % 4, :], RD[:, :], ALU.mult), r)

            def result(i):
                b, j = i // 4, i % 4
                bk, w = take()
                for c in range(4):
                    t_O[b] = op("pe", lambda e, c=c: e.matmul(bank(bk), cT[:, c, 128 * j:128 * j + 128], wout[:, c, :],
                                                              start=(c == 0), stop=(c == 3)), t_nrm[4 * b + 3], taw, *w)
                free[bk] = t_x2[i] = t_xo[i] = op("dve", lambda e: e.tensor_tensor(X[:, i, :], X[:, i, :], bank(bk), ALU.add), t_O[b], t_xz[i])

            stats(0)
            for i in range(4):
                center(i)
                tile(i)
            for u in range(-2, NU + 1):
                now, nxt, far, back = 0 <= u < NU, 0 <= u + 1 < NU, 0 <= u + 2 < NU, 0 <= u - 1 < NU
                if (u + 6) % 4 == 0 and 0 < (u + 6) // 4 < B:
                    stats((u + 6) // 4)
                new = 4 <= u + 6 < NT
                val = 4 <= u + 4 < NT
                b4 = u - 4 if u >= 4 and u % 4 == 0 else None
                ex, sc = 0, 0
                if u == NU - 1:
                    f2["load_router"](t_ST[u - 1])
                    f2["load_shared"](t_ST[u - 1])
                    f2["roots"](0, 12)
                if u == NU:
                    f2["logits"](11)
                for j in range(16):
                    if u == NU - 1 and 2 <= j < 14:
                        f2["tile"](j - 2, t_ST[u - 1], t_Vmm[NT - 1], t_P[NU - 1])
                        if j > 2:
                            f2["logits"](j - 3)
                    if now:
                        while ex < 16 and ex * 14 <= 15 * (j - 1):
                            expo(u, ex)
                            ex += 1
                    if nxt:
                        while sc < 16 and sc * 13 <= 16 * j:
                            scores(u + 1, sc)
                            sc += 1
                    if far and j in (0, 1, 4, 5):
                        project(u + 2, j // 4, j % 4)
                    if far and j in (3, 7):
                        split(u + 2, j // 7)
                    if far and j == 8:
                        stack(u + 2)
                    if u == -2 and j in (8, 9, 10, 11):
                        value(j - 8, 0)
                        value(j - 8, 1)
                    if back and j in (2, 3):
                        weigh(u - 1, 3, j - 2)
                        if j == 3:
                            drain(u - 1)
                    if back and j in (4, 5, 6, 7):
                        norm(u - 1, j - 4)
                    if j == 3:
                        for i in {5: (0, 1), 6: (2, 3), 9: (4, 5), 10: (6, 7), 13: (8, 9), 14: (10, 11)}.get(u, ()):
                            f2["moments"](i)
                    if u == NU and j == 4:
                        f2["shared_up"](0, (0, 1), t_exp[16 * NU - 1])
                    if now and j in (8, 9, 11, 12, 14, 15):
                        weigh(u, (j - 8) // 3, (j - 8) % 3)
                    if val and j in (6, 7):
                        value(u + 4, j - 6)
                    if new and j == 7:
                        center(u + 6)
                    if nxt and j == 13:
                        rows(u + 1)
                    if nxt and j == 14:
                        fill(u + 1)
                    if new and j == 10:
                        tile(u + 6)
                    if b4 is not None and j in (8, 10, 12, 14):
                        result(b4 + (j - 8) // 2)
                        if b4 == NT - 4:
                            f2["moments"](b4 + (j - 8) // 2)
            return t_O[B - 1]

        y_d = nc.dram_tensor("y_d", [T, D], F32, kind="Internal").ap()
        f1 = ffn(0, y_d, [46 + 10 * r for r in range(7)], 35, 36, 116, 156, t_x)
        f1["load_router"]()
        f1["load_shared"](t_x)
        for g in range(3):
            for i in range(4 * g, 4 * g + 4):
                f1["moments"](i)
            f1["roots"](4 * g, 4 * g + 4)
        for i in range(NT):
            if i == 4:
                for k in range(12, NT):
                    f1["moments"](k)
                f1["roots"](12, NT)
            f1["tile"](i)
            if i:
                f1["logits"](i - 1)
        f1["logits"](NT - 1)
        f1["shared_up"](0)
        f1["load_ring"](t_x)
        t_y = f1["rest"]()
        phase()
        s_y = [sem(f"s_yx{g}") for g in range(4)]
        t_x = [dma("sp", f"yx{g}", s_y[g], lambda e, g=g: e.dma_start(
            X[:, 4 * g:4 * g + 4, :], y_d[512 * g:512 * g + 512, :].rearrange("(i p) d -> p i d", p=128)), t_y) for g in range(4)]
        t_x2 = {}
        f2 = ffn(1, o_rows, [46, 36, 107, 117, 127, 137, 147], 66, 56, 67, 157, t_x2)
        t_att = attention([t_x[i // 4] for i in range(NT)], taw, f2, t_x2)
        f2["roots"](12, NT)
        f2["shared_up"](0, (2, 3))
        for i in range(12, NT):
            f2["tile"](i)
            if i > 12:
                f2["logits"](i - 1)
        f2["logits"](NT - 1)
        f2["load_ring"](t_att)
        t_y = f2["rest"]()
        q.wait("pool", t_y)

        block = ctx.enter_context(nc.Block())
        block.sync(lambda e: q.emit("sp", e))
        block.scalar(lambda e: q.emit("act", e))
        block.vector(lambda e: q.emit("dve", e))
        block.gpsimd(lambda e: q.emit("pool", e))
        block.tensor(lambda e: q.emit("pe", e))


_INS = ["L0_attn_X", "L0_attn_ln_w", "L0_attn_ln_b", "L0_attn_W_in", "L0_attn_W_out", "L0_ffn_gate_w", "L0_ffn_bias",
        "L0_ffn_w_gate", "L0_ffn_w_up", "L0_ffn_w_down", "L0_ffn_ws_gate", "L0_ffn_ws_up", "L0_ffn_ws_down"]


def kernel(**inputs):
    import concourse.bacc as bacc
    from concourse.bass_utils import run_bass_kernel_spmd

    nc = bacc.Bacc("TRN2", target_bir_lowering=False, num_devices=1)
    given = {n: np.ascontiguousarray(inputs[n]) for n in _INS}
    given["consts"], given["rope"] = shape_constants()
    arrays, args = {}, []
    for n, a in given.items():
        arrays["in_" + n] = a
        args.append(nc.dram_tensor("in_" + n, a.shape, mybir.dt.from_np(a.dtype), kind="ExternalInput").ap())
    args.append(nc.dram_tensor("out_0", (B, S, D), F32, kind="ExternalOutput").ap())
    macaron_kernel(nc, *args)
    r = run_bass_kernel_spmd(nc, [arrays], core_ids=[0])
    return r.results[0]["out_0"]
```

```python
from contextlib import ExitStack

import concourse.bass as bass
import numpy as np
from concourse import mybir

F32 = mybir.dt.float32
F32R = mybir.dt.float32r
U32 = mybir.dt.uint32
ALU = mybir.AluOpType
ACT = mybir.ActivationFunctionType
AX = mybir.AxisListType.X

D = 512
T = 2048
NT = 16
B = 4
S = 512
NH = 16
DH = 32
E = 64
K = 6
F = 192
FH = 96
CAP = 96
NG = 8
KG = 4
ROW = D + E
EPS = 1e-5
BIG = 3.0e38

C_ID, C_LM, C_IE, C_TK, C_HD, C_N = 0, 128, 192, 256, 272, 400


def shape_constants():
    c = np.zeros((128, C_N), np.float32)
    p = np.arange(128)
    c[:, C_ID:C_ID + 128] = np.eye(128)
    g = np.arange(NG)
    c[:, C_LM:C_LM + 64] = (g[None, :] < g[:, None]).astype(np.float32).reshape(1, 64)
    c[:, C_IE:C_IE + 64] = np.arange(E)[None, :]
    c[:, C_TK:C_TK + 16] = T - (np.arange(NT)[None, :] * 128 + p[:, None])
    c[:4, C_HD:C_HD + 128] = p[:4, None] == p[None, :] // DH
    rot = DH // 2
    inv = (np.float32(1.0) / np.float32(10000.0) ** (np.arange(0, rot, 2, dtype=np.float32) / np.float32(rot))).astype(np.float32)
    ang = np.repeat((np.arange(S, dtype=np.float32)[:, None] * inv[None, :]).astype(np.float32), 2, axis=-1)
    r = np.zeros((DH, 2, S), np.float32)
    r[:, 0, :] = 1.0
    r[:rot, 0, :] = np.cos(ang).T
    r[:rot, 1, :] = np.sin(ang).T * np.where(np.arange(rot) % 2 == 0, -1.0, 1.0)[:, None]
    return c, (np.tile(r, (4, 1, 1)) * np.sqrt(1.0 / np.sqrt(DH))).astype(np.float32)


class Queues:

    def __init__(self, nc, ctx):
        self.items = {n: [] for n in ("pe", "act", "dve", "pool", "sp")}
        self.sem = {n: ctx.enter_context(nc.semaphore("done_" + n)) for n in self.items}
        self.count = dict.fromkeys(self.items, 0)
        self.dma_count = {}
        self.dma_last = {}

    def op(self, eng, fn, *waits):
        self.count[eng] += 1
        self.items[eng].append((fn, waits, self.sem[eng], 1))
        return ("done_" + eng, self.sem[eng], self.count[eng])

    def quiet(self, eng, fn, *waits):
        self.items[eng].append((fn, waits, None, 0))

    def dma(self, eng, name, sem, fn, *waits):
        self.dma_count[name] = self.dma_count.get(name, 0) + 16
        self.items[eng].append((fn, waits, sem, 16))
        self.dma_last[name] = (name, sem, self.dma_count[name])
        return self.dma_last[name]

    def wait(self, eng, *waits):
        self.items[eng].append((None, waits, None, 0))

    def all_done(self):
        return [("done_" + n, self.sem[n], v) for n, v in self.count.items() if v] + list(self.dma_last.values())

    def emit(self, eng, e):
        seen = {}
        for fn, waits, sem, by in self.items[eng]:
            for w in waits:
                for name, s, v in (w if isinstance(w, list) else [w]):
                    if seen.get(name, 0) < v:
                        e.wait_ge(s, v)
                        seen[name] = v
            if fn is not None:
                ins = fn(e)
                if sem is not None:
                    ins.then_inc(sem, by)


def macaron_kernel(nc, X_in, ln_w, ln_b, W_in, W_out, gate_w, bias, w_gate, w_up, w_down,
                   ws_gate, ws_up, ws_down, consts, rope, out):
    x_rows = X_in.rearrange("b s d -> (b s) d")
    o_rows = out.rearrange("b s d -> (b s) d")

    with ExitStack() as ctx:
        base = 16 * 1024 + 128
        names = {}

        def at(name, off, shape, dt=F32):
            names[name] = names.get(name, 0) + 1
            return nc.alloc_sbuf_tensor_at(f"{name}_{names[name]}", shape, dt, offset=base + off)

        def sem(name):
            return ctx.enter_context(nc.semaphore(name))

        KB = 1024
        X = at("X", 0, [128, NT, D])
        cst = at("cst", 32 * KB, [128, C_N])
        biasb = at("biasb", 34 * KB + 512, [128, E])
        lnw = at("lnw", 34 * KB + 768, [128, 4])
        lnb = at("lnb", 34 * KB + 800, [128, 4])
        ident = cst[:, C_ID:C_ID + 128]

        ps = [ctx.enter_context(nc.psum_tensor(f"ps{i}", [128, 2, 512], F32)) for i in range(4)]

        def bank(i):
            return ps[i // 2][:, i % 2, :]

        q = Queues(nc, ctx)
        op, dma = q.op, q.dma

        s_x = [sem(f"s_x{g}") for g in range(4)]
        s_c = sem("s_c")
        s_ln = sem("s_ln")
        s_fw = sem("s_fw")
        s_gw = sem("s_gw")
        s_wqk = [sem(f"s_wqk{j}") for j in range(2)]
        s_wd = sem("s_wd")
        s_aw, s_rp, s_wo = sem("s_aw"), sem("s_rp"), sem("s_wo")
        AW = 156 * KB
        wqk = [at("wqk", AW + 8 * KB * j, [128, 2, 4, 2, 128], F32R) for j in range(2)]
        wv = [at("wv", AW + 16 * KB, [128, 4, D], F32R), at("wv", 131 * KB, [128, 4, D], F32R)]
        wqk_d = nc.dram_tensor("wqk_d", [4, 128, 2, 4, 2, 128], F32, kind="Internal").ap()
        wv_d = nc.dram_tensor("wv_d", [128, 2, 4, D], F32, kind="Internal").ap()
        wout = at("wout", AW + 24 * KB, [128, 4, D])
        rp = at("rp", AW + 32 * KB, [128, 2, S])

        tx = [dma("sp", f"x{g}", s_x[g], lambda e, g=g: e.dma_start(
            X[:, 4 * g:4 * g + 4, :], x_rows[512 * g:512 * g + 512, :].rearrange("(i p) d -> p i d", p=128)))
            for g in range(4)]
        tc = dma("act", "c", s_c, lambda e: e.dma_start(cst[:, :], consts))
        tc = dma("act", "c", s_c, lambda e: e.dma_start(biasb[:, :], bias.partition_broadcast(128)))
        tln = dma("act", "ln", s_ln, lambda e: e.dma_start(lnw[:, :], ln_w.rearrange("(p c) -> p c", c=4)))
        tln = dma("act", "ln", s_ln, lambda e: e.dma_start(lnb[:, :], ln_b.rearrange("(p c) -> p c", c=4)))

        t_x = [tx[i // 4] for i in range(NT)]

        free = [None, None]
        turn = [0]

        def take():
            turn[0] += 1
            j = turn[0] % 2
            return j, ([free[j]] if free[j] else [])

        def rstd(src_var, ve, sq, r, t, wait):
            a = op("dve", lambda e: e.tensor_scalar(ve, src_var, EPS, None, ALU.add), wait)
            return rsqrt(ve, sq, r, t, a)

        def rsqrt(ve, sq, r, t, wait):
            b = op("act", lambda e: e.activation(sq, ve, ACT.Sqrt), wait)
            c = op("dve", lambda e: e.reciprocal(r, sq), b)
            c = op("dve", lambda e: e.tensor_tensor(t, r, r, ALU.mult), c)
            c = op("dve", lambda e: e.tensor_tensor(t, t, ve, ALU.mult), c)
            c = op("dve", lambda e: e.tensor_scalar(t, t, -0.5, 1.5, ALU.mult, ALU.add), c)
            return op("dve", lambda e: e.tensor_tensor(r, r, t, ALU.mult), c)

        def ffn(n, y, ring_at, gw_at, ws_at, A1, A2, t_x):
            NR, NB = 7, 6
            ring = [(at("gu", r * KB, [128, 4, 2, F]), at("wd", (r + 6) * KB, [FH, 2, D])) for r in ring_at + [A2 + 8, A2 + 20]]
            gw = at("gw", gw_at * KB, [128, 4, E])
            wsgu = at("wsgu", ws_at * KB, [128, 4, 2, F])
            wsd = at("wsd", (ws_at + 6) * KB, [128, 2, D])
            A1, A2 = A1 * KB, A2 * KB
            xnT = at("xnT", A1, [128, 4, T])
            XN = at("XN", A1 + 32 * KB, [128, 4, D])
            buf = [at("buf", A1 + j * 2304, [CAP, ROW]) for j in range(NB)]
            o = A1 + NB * 2304
            bufT = [at("bufT", o + j * 1536, [128, 4, CAP]) for j in range(2)]
            sg = [at("sg", o + 3072 + j * 768, [FH, 2, CAP]) for j in range(2)]
            hH = [at("hH", o + 4608 + j * 768, [FH, 2, CAP], F32R) for j in range(2)]
            hL = [at("hL", o + 12288 + j * 768, [FH, 2, CAP], F32R) for j in range(2)]
            hF = [at("hF", o + 13824 + j * 768, [FH, 2, CAP]) for j in range(2)]
            osb = [at("osb", o + 6144 + j * 2048, [CAP, D]) for j in range(3)]
            R = [at(f"R{j}", A2 + 4 * KB * j, [128, NT, E]) for j in range(7)]
            wdH = [at("wdH", v, [FH, 2, D], F32R) for v in (A1 + 32 * KB, A2 + 36 * KB)]
            wdL = [at("wdL", v, [FH, 2, D], F32R) for v in (A1 + 36 * KB, A2 + 40 * KB)]
            keyT = at("keyT", A2 + 32 * KB, [128, T // 2])
            sgs = at("sgs", A2 + 36 * KB, [FH, 2, S])
            hTs = [at("hTs", A2 + 40 * KB, [FH, 2, S]), at("hTs", A2 + 4 * KB, [FH, 2, S])]
            A3 = A2 + 44 * KB
            A4 = 207 * KB - 256
            BS = at("BS", A4, [128, NT, 6])
            MV = at("MV", A4 + 384, [128, NT, 2])
            VE, SQ, RS, TM = [at("sm", A4 + 512 + 64 * j, [128, NT]) for j in range(4)]
            V8 = at("V8", A3 + 768, [128, NT, 8])
            I8 = at("I8", A3 + 1280, [128, NT, 8], U32)
            i6 = at("i6", A3 + 2304, [128, NT])
            den = at("den", A3 + 2368, [128, NT])
            lst = at("lst", A3 + 2432, [128, CAP])
            cand = at("cand", A3 + 2816, [E, 2 * CAP])
            first = at("first", A3 + 3584, [E, CAP])
            tok = at("tok", A3 + 3968, [CAP, E], U32)
            tokf = at("tokf", A3 + 4224, [CAP, E])
            assert A3 + 4480 <= A4

            xn_d = nc.dram_tensor(f"xn_d{n}", [T, ROW], F32, kind="Internal").ap()
            s_ring = [sem(f"s_ring{n}_{r}") for r in range(NR + 2)]
            s_xn = [sem(f"s_xn{n}_{r}") for r in range(4)]
            s_w = sem(f"s_w{n}")
            s_buf = [sem(f"s_buf{n}_{r}") for r in range(NB)]
            s_out = sem(f"s_out{n}")
            s_y = sem(f"s_y{n}")

            def slot(x):
                return x if x < NR + 2 else (x - NR - 2) % NR

            def load(x, *waits):
                gu, wd = ring[slot(x)]
                nm, s = f"ring{n}_{slot(x)}", s_ring[slot(x)]
                dma("sp", nm, s, lambda e: e.dma_start(gu[:, :, 0, :], w_gate[x].rearrange("(p c) f -> p c f", c=4)), *waits)
                dma("sp", nm, s, lambda e: e.dma_start(gu[:, :, 1, :], w_up[x].rearrange("(p c) f -> p c f", c=4)))
                return dma("sp", nm, s, lambda e: e.dma_start(wd[:, :, :], w_down[x].rearrange("(c p) h -> p c h", c=2)))

            tgw, tfw = [], []

            def load_router(*waits):
                tgw.append(dma("sp", "gw", s_gw, lambda e: e.dma_start(gw[:, :, :], gate_w.rearrange("(p c) n -> p c n", c=4)), *waits))

            def load_shared(*waits):
                dma("sp", "fw", s_fw, lambda e: e.dma_start(wsgu[:, :, 0, :], ws_gate.rearrange("(p c) n -> p c n", c=4)), *waits)
                dma("sp", "fw", s_fw, lambda e: e.dma_start(wsgu[:, :, 1, :], ws_up.rearrange("(p c) n -> p c n", c=4)))
                tfw.append(dma("sp", "fw", s_fw, lambda e: e.dma_start(wsd[0:FH, :, :], ws_down.rearrange("(c p) n -> p c n", c=2))))

            tr, tt, t_evT, t_lg, t_xnd, t_ring = {}, {}, {}, {}, {}, {}

            def moments(i):
                t = op("dve", lambda e: e.bn_stats(BS[:, i, :], X[:, i, :]), t_x[i])
                tr[i] = op("dve", lambda e: e.bn_aggr(MV[:, i, :], BS[:, i, :]), t)

            def roots(lo, hi):
                gs = slice(lo, hi)
                t = rstd(MV[:, gs, 1], VE[:, gs], SQ[:, gs], RS[:, gs], TM[:, gs], tr[hi - 1])
                for i in range(lo, hi):
                    tr[i] = t

            def tile(i, eng, *waits):
                w = [t_evT[i - 4], t_xnd[i - 4]] if i >= 4 else []
                tn = op(eng, lambda e: e.tensor_scalar(XN[:, i % 4, :], X[:, i, :], MV[:, i, 0:1], RS[:, i:i + 1],
                                                         ALU.subtract, ALU.mult), tr[i], *w)
                t_xnd[i] = dma("sp", f"xn{n}_{i % 4}", s_xn[i % 4], lambda e: e.dma_start(
                    xn_d[128 * i:128 * i + 128, 0:D], XN[:, i % 4, :]), tn)
                bk, w = take()
                for c in range(4):
                    tt[i] = op("pe", lambda e, c=c: e.transpose(bank(bk)[:, 128 * c:128 * c + 128], XN[:, i % 4, c:D:4], ident),
                               tn, tc, *w)
                free[bk] = t_evT[i] = op("act", lambda e: e.copy(xnT[:, :, 128 * i:128 * i + 128],
                                                                 bank(bk).rearrange("p (c t) -> p c t", c=4)), tt[i], *waits)

            def logits(i):
                for c in range(4):
                    t_lg[i] = op("pe", lambda e, c=c: e.matmul(
                        bank(4 + i // 8)[:, 64 * (i % 8):64 * (i % 8) + 64],
                        xnT[:, c, 128 * i:128 * i + 128], gw[:, c, :], start=(c == 0), stop=(c == 3)), t_evT[i], tgw)

            def load_ring(xs, *waits):
                for x in xs:
                    t_ring[x] = load(x, *waits)

            t_hs, t_up = {}, {}

            def shared_up(gq, js=range(4), *waits):
                w = [t_hs[gq - 1]] if gq else []
                for j in js:
                    for c in range(4):
                        t_up[gq] = op("pe", lambda e, j=j, c=c: e.matmul(
                            bank(2 + j if j < 2 else 4 + j)[0:FH, :], wsgu[:, c, j // 2, FH * (j % 2):FH * (j % 2) + FH],
                            xnT[:, c, S * gq:S * gq + S], start=(c == 0), stop=(c == 3)), tfw, t_evT[4 * gq + 3], *w, *waits)

            def rest(aside=lambda: None):
                t_sh, t_dn, t_shc, w_out = {}, {}, {}, []

                t_si = {}

                def shared_silu(gq):
                    w = [t_hs[gq - 1]] if gq else []
                    t_si[gq] = op("act", lambda e: e.activation(sgs[:, :, :], ps[1][0:FH, :, :], ACT.Silu), t_up[gq], *w)

                def shared_mul(gq, *waits):
                    w = [t_dn[gq - 2]] if gq >= 2 else []
                    t_hs[gq] = op("dve", lambda e: e.tensor_tensor(hTs[gq % 2][:, :, :], sgs[:, :, :], ps[3][0:FH, :, :], ALU.mult), t_si[gq], *w, *waits)

                def shared_down(gq):
                    for j in range(4):
                        i = 4 * gq + j
                        w = [t_shc[i - 2]] if i >= 2 else [t_evT[NT - 1]]
                        for h in range(2):
                            t_dn[gq] = op("pe", lambda e, j=j, i=i, h=h: e.matmul(
                                bank(i % 2), hTs[gq % 2][:, h, 128 * j:128 * j + 128], wsd[0:FH, h, :],
                                start=(h == 0), stop=(h == 1)), t_hs[gq], *w)
                        w = [t_sh[i - 4]] if i >= 4 else [t_xnd[NT - 4 + i]]
                        t_shc[i] = op("act", lambda e, i=i: e.activation(XN[:, i % 4, :], bank(i % 2), ACT.Copy, scale=0.5), t_dn[gq], *w)
                        t_sh[i] = op("pool", lambda e, i=i: e.tensor_tensor(X[:, i, :], X[:, i, :], XN[:, i % 4, :], ALU.add), t_shc[i])
                        w_out.append(dma("act", f"y{n}", s_y, lambda e, i=i: e.dma_start(y[128 * i:128 * i + 128, :], X[:, i, :]), t_sh[i]))

                SC, SB, P1, P2, SEL, W, P3 = [r[:, :, :] for r in R]
                flat = lambda ap: ap.rearrange("p i e -> p (i e)")
                grp = lambda ap: ap.rearrange("p i (g j) -> p (i g) j", j=8)
                bE = lambda ap: ap.unsqueeze(2).to_broadcast([128, NT, E])
                cE = lambda o: cst[:, o:o + 64].unsqueeze(1).to_broadcast([128, NT, E])
                dv = lambda fn, *w: op("dve", fn, *w)
                TT = lambda o, a, b, f: (lambda e: e.tensor_tensor(o, a, b, f))

                t_sc = op("act", lambda e: e.activation(SC.rearrange("p (a i) e -> p a (i e)", a=2), ps[2][:, :, :], ACT.Sigmoid), t_lg[NT - 1])
                ahead = n

                def shared_step(k, *waits):
                    if k < 4:
                        shared_mul(k, *waits)
                    if k + 1 < 4:
                        shared_up(k + 1)
                        shared_silu(k + 1)

                shared_silu(0)
                aside()
                if ahead:
                    shared_step(0)
                t = dv(TT(SB, SC, biasb[:, :].unsqueeze(1).to_broadcast([128, NT, E]), ALU.add), t_sc, tc)
                s8 = grp(SB)
                part = lambda ap, o, m, j: flat(ap)[:, o:o + m * j].rearrange("p (m j) -> p m j", j=j)
                h1, l1 = part(P1, 0, 128, 4), part(P1, 512, 128, 4)
                h2, l2, u2 = part(P2, 0, 128, 2), part(P2, 256, 128, 2), part(P2, 512, 128, 2)
                h3, l3, u3, gsum, rank, msk, neg = (flat(P3)[:, 128 * j:128 * j + 128] for j in range(7))
                dv(TT(h1, s8[:, :, 0::2], s8[:, :, 1::2], ALU.max), t)
                t = dv(TT(l1, s8[:, :, 0::2], s8[:, :, 1::2], ALU.min), t)
                dv(TT(h2, h1[:, :, 0::2], h1[:, :, 1::2], ALU.max), t)
                dv(TT(l2, h1[:, :, 0::2], h1[:, :, 1::2], ALU.min), t)
                t = dv(TT(u2, l1[:, :, 0::2], l1[:, :, 1::2], ALU.max), t)
                t = dv(TT(l2, l2, u2, ALU.max), t)
                dv(TT(h3, h2[:, :, 0], h2[:, :, 1], ALU.max), t)
                dv(TT(l3, h2[:, :, 0], h2[:, :, 1], ALU.min), t)
                t = dv(TT(u3, l2[:, :, 0], l2[:, :, 1], ALU.max), t)
                t = dv(TT(l3, l3, u3, ALU.max), t)
                t = dv(TT(gsum, h3, l3, ALU.add), t)
                G3 = gsum.rearrange("p (i g) -> p i g", g=NG)
                ga = G3.unsqueeze(2).to_broadcast([128, NT, NG, NG])
                gb = G3.unsqueeze(3).to_broadcast([128, NT, NG, NG])
                r4 = lambda ap: ap.rearrange("p i (g j) -> p i g j", j=NG)
                dv(TT(r4(P1), ga, gb, ALU.is_gt), t)
                t = dv(TT(r4(P2), ga, gb, ALU.is_equal), t)
                t = dv(TT(P2, P2, cE(C_LM), ALU.mult), t)
                t = dv(TT(P1, P1, P2, ALU.add), t)
                t = dv(lambda e: e.tensor_reduce(rank, grp(P1), AX, ALU.add), t)
                t = dv(lambda e: e.tensor_scalar(msk, rank, float(KG), None, ALU.is_lt), t)
                t = dv(lambda e: e.tensor_scalar(neg, msk, BIG, -BIG, ALU.mult, ALU.add), t)
                bg = lambda ap: ap.unsqueeze(2).to_broadcast([128, 128, 8])
                t = dv(TT(grp(P1), s8, bg(neg), ALU.add), t)
                shared_step(ahead, t)
                for i in range(NT):
                    tv = dv(lambda e, i=i: e.max(V8[:, i, :], P1[:, i, :]), t)
                tk = cst[:, C_TK:C_TK + 16].unsqueeze(2).to_broadcast([128, NT, E])
                a = dv(TT(P3, P1, bE(V8[:, :, K - 1]), ALU.is_gt), tv)
                a2 = op("pool", lambda e: e.tensor_scalar(W, P3, float(T), None, ALU.mult), a)
                g = op("pool", TT(W, W, tk, ALU.add), a2)
                for i in range(NT):
                    ti = dv(lambda e, i=i: e.max_index(I8[:, i, :], V8[:, i, :], P1[:, i, :]), tv)
                t = dv(lambda e: e.tensor_copy(i6[:, :], I8[:, :, K - 1]), ti)
                dv(TT(SEL, P1, bE(V8[:, :, K - 1]), ALU.is_equal), tv)
                t = dv(TT(P2, cE(C_IE), bE(i6[:, :]), ALU.is_le), t)
                t_eq = dv(TT(P2, P2, SEL, ALU.mult), t)
                t_key = dv(lambda e: e.scalar_tensor_tensor(out=P1, in0=P2, scalar=float(T), in1=W, op0=ALU.mult, op1=ALU.add), t_eq, g)
                for i in range(8):
                    tp = op("pe", lambda e, i=i: e.transpose(bank(4 + i // 4)[:, 128 * (i % 4):128 * (i % 4) + 128],
                                                             flat(P1)[:, 128 * i:128 * i + 128], ident), t_key, t_sc)
                shared_down(0)
                t = op("pool", TT(SEL, P2, P3, ALU.add), t_eq, a)
                t_sel = op("pool", TT(P2, SC, SEL, ALU.mult), t)

                def weights():
                    t = dv(lambda e: e.tensor_reduce(den[:, :], P2, AX, ALU.add), t_sel)
                    t = dv(lambda e: e.reciprocal(den[:, :], den[:, :]), t)
                    t = dv(lambda e: e.tensor_scalar(den[:, :], den[:, :], 1.25, None, ALU.mult), t)
                    t = op("pool", TT(W, P2, bE(den[:, :]), ALU.mult), t)
                    return dma("act", f"w{n}", s_w, lambda e: e.dma_start(xn_d[:, D:ROW].rearrange("(i p) e -> p i e", p=128), W), t)

                if not ahead:
                    shared_step(1)
                    shared_down(1)
                t, src = tp, ps[2][:, :, :].rearrange("p a b -> p (a b)")
                for r in range(CAP // 8):
                    t = dv(lambda e, r=r, src=src: e.max(lst[:, 8 * r:8 * r + 8], src), t)
                    if r < CAP // 8 - 1:
                        t = t_kT = dv(lambda e, r=r, src=src: e.match_replace(keyT[:, :], lst[:, 8 * r:8 * r + 8], src, 0.0), t)
                    src = keyT[:, :]
                    if r == 5:
                        t_wd = weights()
                        for x in (NR, NR + 1):
                            t_ring[x] = load(x, tp, t_wd)
                    if r == 2 and ahead:
                        shared_step(2)
                        shared_down(1)
                    if r == 6 and not ahead:
                        shared_step(2)
                    if r == 11 and ahead:
                        shared_step(3)
                        shared_down(2)
                dv(lambda e: e.tensor_copy(cand[:, 0:CAP], lst[0:E, :]), t)
                t = dv(lambda e: e.tensor_copy(cand[:, CAP:2 * CAP], lst[E:128, :]), t)
                for r in range(CAP // 8):
                    t = dv(lambda e, r=r: e.max(first[:, 8 * r:8 * r + 8], cand[:, :]), t)
                    if r < CAP // 8 - 1:
                        t = dv(lambda e, r=r: e.match_replace(cand[:, :], first[:, 8 * r:8 * r + 8], cand[:, :], 0.0), t)
                tp = op("pe", lambda e: e.transpose(bank(4)[0:CAP, 0:E], first[:, :], cst[0:E, C_ID:C_ID + E]), t, t_kT)
                t = dv(lambda e: e.tensor_scalar(tokf[:, :], bank(4)[0:CAP, 0:E], float(T), float(T), ALU.is_gt, ALU.mult), tp)
                t_tok = dv(lambda e: e.scalar_tensor_tensor(out=tok[:, :], in0=tokf[:, :], scalar=float(T), in1=bank(4)[0:CAP, 0:E],
                                                            op0=ALU.add, op1=ALU.subtract), t)
                if not ahead:
                    shared_step(3)

                t_buf, t_bT, t_gu, t_h, t_wL, t_d, t_ev, t_out = {}, {}, {}, {}, {}, {}, {}, {}

                def gather(x):
                    w = [t_ev[x - NB]] if x >= NB else [t_tok, t_wd, t_up[3]] + [t_xnd[i] for i in range(NT - 4, NT)]
                    t_buf[x] = dma("pool", f"buf{n}_{x % NB}", s_buf[x % NB], lambda e: e.indirect_dma_start(
                        out=buf[x % NB][:, :], out_offset=None, in_=xn_d, in_offset=bass.IndirectOffsetOnAxis(ap=tok[:, x:x + 1], axis=0),
                        bounds_check=T - 1, oob_is_err=True), *w)

                for x in range(NB):
                    gather(x)
                if not ahead:
                    shared_down(2)
                shared_down(3)
                for st in range(E + 2):
                    x = st
                    if x < E:
                        w = [t_bT[x - 2]] if x >= 2 else [t_shc[NT - 1]]
                        for c in range(4):
                            tt = op("pe", lambda e, x=x, c=c: e.transpose(bank(x % 2)[:, CAP * c:CAP * c + CAP],
                                                                          buf[x % NB][:, c:D:4], cst[0:CAP, C_ID:C_ID + CAP]), t_buf[x], *w)
                        w = [t_gu[x - 2]] if x >= 2 else []
                        t_bT[x] = op("act", lambda e, x=x: e.copy(bufT[x % 2][:, :, :], bank(x % 2)[:, 0:4 * CAP].rearrange("p (c t) -> p c t", c=4)), tt, *w)
                    x = st - 1
                    if 0 <= x < E:
                        gu, wd = ring[slot(x)]
                        w = [t_h[x - 2]] if x >= 2 else [t_hs[3]]
                        for j in range(4):
                            for c in range(4):
                                t_gu[x] = op("pe", lambda e, x=x, gu=gu, j=j, c=c: e.matmul(
                                    bank(2 + x % 2)[0:FH, CAP * j:CAP * j + CAP], gu[:, c, j // 2, FH * (j % 2):FH * (j % 2) + FH],
                                    bufT[x % 2][:, c, :], start=(c == 0), stop=(c == 3)), t_bT[x], t_ring[x], *w)
                        w = [t_h[x - 2]] if x >= 2 else []
                        a = op("act", lambda e, x=x: e.activation(sg[x % 2][:, :, :].rearrange("p a b -> p (a b)"),
                                                                  bank(2 + x % 2)[0:FH, 0:2 * CAP], ACT.Silu), t_gu[x], *w)
                        fl = lambda v: v.rearrange("p a b -> p (a b)")
                        w = [t_d[x - 2]] if x >= 2 else []
                        m = op("dve", lambda e, x=x: e.tensor_tensor(fl(hF[x % 2][:, :, :]), fl(sg[x % 2][:, :, :]),
                                                                     bank(2 + x % 2)[0:FH, 2 * CAP:4 * CAP], ALU.mult), a, *w)
                        a = op("act", lambda e, x=x: e.copy(hH[x % 2][:, :, :], hF[x % 2][:, :, :]), m, *w)
                        w += [t_sh[NT - 1], t_dn[3], t_ring[x]]
                        b = op("act", lambda e, x=x, wd=wd: e.copy(wdH[x % 2][:, :, :], wd[:, :, :]), *w)
                        t_wL[x] = op("dve", lambda e, x=x, wd=wd: e.tensor_tensor(wdL[x % 2][:, :, :], wd[:, :, :], wdH[x % 2][:, :, :].bitcast(F32), ALU.subtract), b)
                        t_h[x] = op("dve", lambda e, x=x: e.tensor_tensor(hL[x % 2][:, :, :], hF[x % 2][:, :, :], hH[x % 2][:, :, :].bitcast(F32), ALU.subtract), a)
                    x = st - 2
                    if 0 <= x < E:
                        w = [t_ev[x - 2]] if x >= 2 else [t_tok]
                        hw = [(hH, wdH), (hH, wdL), (hL, wdH)]
                        for h in range(2):
                            for k, (u, v) in enumerate(hw):
                                t_d[x] = op("pe", lambda e, x=x, h=h, k=k, u=u, v=v: e.matmul(
                                    bank(4 + x % 2)[0:CAP, :], u[x % 2][:, h, :], v[x % 2][:, h, :],
                                    start=(h == 0 and k == 0), stop=(h == 1 and k == 2)), t_h[x], t_wL[x], *w)
                        w = [t_out[x - 3]] if x >= 3 else []
                        t_ev[x] = op("dve", lambda e, x=x: e.tensor_scalar(osb[x % 3][:, :], bank(4 + x % 2)[0:CAP, :],
                                                                           buf[x % NB][:, D + x:D + x + 1], None, ALU.mult), t_d[x], *w)
                        if x + NB < E:
                            gather(x + NB)
                        t_out[x] = dma("pool", f"out{n}", s_out, lambda e, x=x: e.indirect_dma_start(
                            out=y, out_offset=bass.IndirectOffsetOnAxis(ap=tok[:, x:x + 1], axis=0), in_=osb[x % 3][:, :], in_offset=None,
                            bounds_check=T - 1, oob_is_err=True, compute_op=ALU.add), t_ev[x], *(w_out[-1:] if x == 0 else [t_out[x - 1]]))
                        after = x + NR + 2 if x < NR else x + NR
                        if after < E and not NR <= x < NR + 2:
                            t_ring[after] = load(after, t_d[x])

                return t_out[E - 1]

            return dict(load_router=load_router, load_shared=load_shared, load_ring=load_ring, moments=moments, roots=roots,
                        tile=tile, logits=logits, shared_up=shared_up, rest=rest)

        def phase():
            done = q.all_done()
            for n in q.items:
                q.wait(n, done)

        def fetch(u, *waits):
            return dma("sp", f"wqk{u % 2}", s_wqk[u % 2], lambda e: e.dma_start(
                wqk[u % 2][:, :, :, :, :].bitcast(F32).rearrange("p a c k n -> p (a c k n)"),
                wqk_d[u % 4].rearrange("p a c k n -> p (a c k n)")), *waits)

        def attention(t_x, twv, trp, two, t_w, f2, t_x2):
            AT = 35 * KB
            St = [at("St", AT + 16 * KB * j, [98, 2, 4, S], F32R) for j in range(3)]
            xT = [at("xT", AT + 48 * KB + 8 * KB * j, [128, 4, S], F32R) for j in range(2)]
            V = [at("V", AT + 64 * KB + 8 * KB * j, [128, 4, D]) for j in range(2)]
            NP = 8
            PT = [at("PT", AT + 80 * KB + 2 * KB * j, [128, S]) for j in range(NP)]
            HL = at("HL", AT + 104 * KB, [128, 4, S], F32R)
            hi = lambda k: HL[:, 1 + k, :]
            lo = lambda k: HL[:, 3 * k, :].bitcast(F32)
            cT = at("cT", AT + 112 * KB, [128, 4, S])
            o = AW + 36 * KB
            mh = at("mh", o, [4, 2, S], F32R)
            t2 = at("t2", o + 4 * KB, [128, 2, S])
            ZH = at("ZH", o + 8 * KB, [128, D])
            xF = at("xF", o + 10 * KB, [128, 4, 128])
            rd = at("rd", o + 12 * KB, [4, S])
            o += 14 * KB
            Dn = at("Dn", o, [128, 4, 4])
            Rn = [at("Rn", o + 64 * (j + 1), [128, 4, 4]) for j in range(2)]
            Mx = at("Mx", o + 192, [128, 4, 4])
            BS = at("BS", o + 256, [128, 4, 6])
            MV = at("MV", o + 352, [128, NT, 2])
            RS = at("RS", o + 480, [128, 2, NT])[:, :, :]
            OP, NM = [at("sm", o + 608 + 64 * j, [128, NT])[:, :] for j in range(2)]
            VE, SQ, TM = [at("sm", AW + 48 * KB + 128 * j, [128, 2, NT])[:, :, :] for j in range(3)]
            s_st = [[sem(f"s_st{j}_{h}") for h in range(4)] for j in range(3)]
            s_m = [sem(f"s_m{j}") for j in range(3)]
            NU = 4 * B

            for j in range(3):
                t_st1 = op("pool", lambda e, j=j: e.memset(St[j][96:98, 1, :, :].bitcast(F32), 1.0))
            q.wait("pool", t_st1)

            t_stat, t_xT, t_V, t_hl, t_st, t_max, t_md, t_rows = {}, {}, {}, {}, {}, {}, {}, {}
            t_tt, t_mv, t_xF = {}, {}, {}
            t_zh, t_xz, t_P, t_ST, t_exp, t_pv, t_nrm, t_O, t_xo, t_Vmm = {}, {}, {}, {}, {}, {}, {}, {}, {}, {}
            got = lambda d, k: [d[k]] if k in d else []

            def stats(lo, hi):
                for i in range(lo, hi):
                    t = op("dve", lambda e, i=i: e.bn_stats(BS[:, i % 4, :], X[:, i, :]), t_x[i], *got(t_mv, i - 4))
                    t = t_mv[i] = op("dve", lambda e, i=i: e.bn_aggr(MV[:, i, :], BS[:, i % 4, :]), t)
                g = slice(lo, hi)
                op("dve", lambda e: e.tensor_scalar(VE[:, 0, g], MV[:, g, 1], EPS, None, ALU.add), t)
                t = op("dve", lambda e: e.tensor_scalar(VE[:, 1, g], MV[:, g, 1], 1.0 + EPS, EPS * EPS, ALU.mult, ALU.add), t)
                t = rsqrt(VE[:, :, g], SQ[:, :, g], RS[:, :, g], TM[:, :, g], t)
                op("dve", lambda e: e.tensor_scalar(OP[:, g], RS[:, 0, g], 1.0, None, ALU.add), t)
                t = op("dve", lambda e: e.scalar_tensor_tensor(out=NM[:, g], in0=MV[:, g, 0], scalar=-1.0, in1=RS[:, 0, g], op0=ALU.mult, op1=ALU.mult), t)
                for i in range(lo, hi):
                    t_stat[i] = t

            def center(i):
                z = ZH
                t_zh[i] = op("dve", lambda e: e.tensor_scalar(z[:, :], X[:, i, :], MV[:, i, 0:1], RS[:, 1, i:i + 1], ALU.subtract, ALU.mult),
                             t_stat[i], *got(t_tt, i - 1))

            def residual(i):
                t_xz[i] = op("pool", lambda e: e.tensor_scalar(X[:, i, :], X[:, i, :], OP[:, i:i + 1], NM[:, i:i + 1], ALU.mult, ALU.add), t_zh[i])

            def tile(i):
                bk, w = take()
                for c in range(4):
                    t_tt[i] = op("pe", lambda e, c=c: e.transpose(bank(bk)[:, 128 * c:128 * c + 128], ZH[:, c:D:4], ident), t_zh[i], *w)
                for c in range(4):
                    free[bk] = t_xF[i] = op("act", lambda e, c=c: e.activation(
                        xF[:, c, :], bank(bk)[:, 128 * c:128 * c + 128], ACT.Identity,
                        bias=lnb[:, c:c + 1], scale=lnw[:, c:c + 1]), t_tt[i], tln, *got(t_xT, i - 1))

            def halve(i):
                b, cols = i // 4, slice(128 * (i % 4), 128 * (i % 4) + 128)
                h = op("dve", lambda e: e.tensor_copy(xT[0][:, :, cols], xF[:, :, :]), t_xF[i], *got(t_P, 4 * b - 1), *got(t_Vmm, 4 * b - 1))
                t_xT[i] = op("dve", lambda e: e.tensor_tensor(xT[1][:, :, cols], xF[:, :, :], xT[0][:, :, cols].bitcast(F32), ALU.subtract), h)

            held, t_dr, t_mh, t_den, t_inv, t_tr, t_rd, t_bc = {}, {}, {}, {}, {}, {}, {}, {}

            def value(i, half):
                b, j = i // 4, i % 4
                if half == 0:
                    held["V"] = take()
                bk, w = held["V"]
                for c in (2 * half, 2 * half + 1):
                    for k, (x, y) in enumerate(parts):
                        t_Vmm[i] = op("pe", lambda e, c=c, k=k, x=x, y=y: e.matmul(
                            bank(bk), xT[y][:, c, 128 * j:128 * j + 128], wv[x][:, c, :],
                            start=(c == 0 and k == 0), stop=(c == 3 and k == 2)), t_xT[i], twv, *w)
                if half:
                    t_V[i] = op("dve", lambda e: e.tensor_copy(V[b % 2][:, j, :], bank(bk)), t_Vmm[i], *got(t_pv, (4 * b - 5, 3)))
                    free[bk] = t_V[i]

            parts = ((0, 0), (0, 1), (1, 0))

            def project(u, k, half):
                b = u // 4
                if half == 0:
                    held["P"] = take()
                bk, w = held["P"]
                for c in (2 * half, 2 * half + 1):
                    for m, (x, y) in enumerate(parts):
                        t_P[u] = op("pe", lambda e, c=c, m=m, x=x, y=y: e.matmul(
                            bank(bk), wqk[u % 2][:, x, c, k, :], xT[y][:, c, :],
                            start=(c == 0 and m == 0), stop=(c == 3 and m == 2)), t_xT[4 * b + 3], t_w[u], *w)
                if not half:
                    return
                w = got(t_st, u - 1)
                a = op("dve", lambda e: e.stream_shuffle(t2[:, k, :], bank(bk), [i ^ 1 for i in range(32)]), t_P[u], *got(t_hl, (u - 1, k)))
                a = op("pool", lambda e: e.tensor_tensor(t2[:, k, :], t2[:, k, :], rp[:, 1, :], ALU.mult), a, trp)
                free[bk] = d = op("dve", lambda e: e.tensor_tensor(lo(k), bank(bk), rp[:, 0, :], ALU.mult), t_P[u], trp, *w)
                t_hl[u, k] = op("pool", lambda e: e.tensor_tensor(lo(k), lo(k), t2[:, k, :], ALU.add), d, a)

            def split(u, k):
                h = op("act", lambda e: e.copy(hi(k), lo(k)), t_hl[u, k], *got(t_st, u - 1))
                t_hl[u] = op("pool", lambda e: e.tensor_tensor(HL[:, 3 * k, :], lo(k), hi(k).bitcast(F32), ALU.subtract), h)

            def stack(u):
                d = St[u % 3]
                w = got(t_ST, u - 3)
                t_st[u] = []
                for j in range(4):
                    for s_, x in enumerate((slice(1, 3), slice(1, 4, 2), slice(0, 3, 2))):
                        t = dma("sp", f"st{u % 3}_{j}", s_st[u % 3][j], lambda e, j=j, s_=s_, x=x: e.dma_start(
                            d[32 * s_:32 * s_ + 32, :, j, :].bitcast(F32), HL[32 * j:32 * j + 32, x, :].bitcast(F32)), t_hl[u], *w)
                    t_st[u].append(t)

            def scores(u, j):
                d, hl, qt = St[u % 3], j // 4, j % 4
                n = 16 * u + j
                bk = (4, 5, 7)[n % 3]
                t = op("pe", lambda e: e.matmul(bank(bk), d[0:96, 0, hl, 128 * qt:128 * qt + 128], d[0:96, 1, hl, :],
                                                start=True, stop=True), t_st[u][hl], *got(t_den, n - 3))
                t_max[n] = op("dve", lambda e: e.tensor_reduce(Mx[:, qt, hl:hl + 1], bank(bk), AX, ALU.max, negate=True),
                              t, *got(t_rows, u - 1), *got(t_den, 16 * u - 1))
                t_den[n] = op("act", lambda e: e.activation(bank(bk), bank(bk), ACT.Exp, bias=Mx[:, qt, hl:hl + 1],
                                                            accum_out=Dn[:, qt, hl:hl + 1]), t_max[n], *got(t_inv, u - 1))

            def invert(u):
                t_inv[u] = op("dve", lambda e: e.reciprocal(Rn[u % 2][:, :, :], Dn[:, :, :]), t_den[16 * u + 15], *got(t_tr, u - 2))

            def spread(u):
                bk, w = take()
                for qt in range(4):
                    t_tr[u] = op("pe", lambda e, qt=qt: e.transpose(bank(bk)[0:4, 128 * qt:128 * qt + 128], Rn[u % 2][:, qt, :], ident), t_inv[u], *w)
                free[bk] = t_rd[u] = op("act", lambda e: e.copy(rd[:, :], bank(bk)[0:4, :]), t_tr[u], *got(t_bc, u - 1))

            def broadcast(u):
                bk, w = take()
                t_bc[u] = op("pe", lambda e: e.matmul(bank(bk), cst[0:4, C_HD:C_HD + 128], rd[:, :], start=True, stop=True), t_rd[u], *w)
                free[bk] = t_nrm[u] = op("dve", lambda e: e.tensor_tensor(cT[:, u % 4, :], cT[:, u % 4, :], bank(bk), ALU.mult), t_bc[u], t_dr[u])

            def rows(u):
                bk, w = take()
                for qt in range(4):
                    t_rows[u] = op("pe", lambda e, qt=qt: e.transpose(bank(bk)[0:4, 128 * qt:128 * qt + 128], Mx[:, qt, :], ident),
                                   t_max[16 * u + 15], *w)
                a = op("act", lambda e: e.copy(mh[:, 0, :], bank(bk)[0:4, :]), t_rows[u], *got(t_md, u - 1))
                free[bk] = t_mh[u] = op("dve", lambda e: e.tensor_tensor(mh[:, 1, :], bank(bk)[0:4, :], mh[:, 0, :].bitcast(F32), ALU.subtract), a)

            def fill(u):
                for j in range(2):
                    t_md[u] = dma("act", f"m{u % 3}", s_m[u % 3], lambda e, j=j: e.dma_start(
                        St[u % 3][96 + j:97 + j, 0, :, :].bitcast(F32), mh[:, j, :].bitcast(F32)), t_mh[u], *got(t_ST, u - 3))

            def expo(u, j):
                d, hl, kt = St[u % 3], j % 4, j // 4
                n = 16 * u + j
                bk = 2 + j % 2
                t_ST[u] = op("pe", lambda e: e.matmul(bank(bk), d[0:98, 1, hl, 128 * kt:128 * kt + 128], d[0:98, 0, hl, :],
                                                      start=True, stop=True), t_st[u], t_md[u], t_st1, *got(t_exp, n - 2))
                m = n - NP
                t_exp[n] = op("act", lambda e: e.activation(PT[n % NP][:, :], bank(bk), ACT.Exp), t_ST[u],
                              *(got(t_pv, (m // 16, m % 16 // 4)) if m >= 0 else []))

            def weigh(u, kt):
                b = u // 4
                for hl in range(4):
                    n = 16 * u + 4 * kt + hl
                    h = 4 * (u % 4) + hl
                    t_pv[u, kt] = op("pe", lambda e, hl=hl, n=n, h=h: e.matmul(
                        bank(6)[32 * hl:32 * hl + 32, :], V[b % 2][:, kt, DH * h:DH * h + DH], PT[n % NP][:, :], start=(kt == 0), stop=(kt == 3),
                        tile_position=(0, 32 * hl), skip_group_check=True),
                        t_exp[n], t_V[4 * b + kt], *got(t_dr, u - 1))

            def drain(u):
                t_dr[u] = op("act", lambda e: e.copy(cT[:, u % 4, :], bank(6)), t_pv[u, 3], *got(t_O, u // 4 - 1))

            def result(i):
                b, j = i // 4, i % 4
                bk, w = take()
                for c in range(4):
                    t_O[b] = op("pe", lambda e, c=c: e.matmul(bank(bk), cT[:, c, 128 * j:128 * j + 128], wout[:, c, :],
                                                              start=(c == 0), stop=(c == 3)), t_nrm[4 * b + 3], two, *w)
                free[bk] = t_x2[i] = t_xo[i] = op("dve", lambda e: e.tensor_tensor(X[:, i, :], X[:, i, :], bank(bk), ALU.add), t_O[b], t_xz[i])

            stats(0, 4)
            for i in range(4):
                center(i)
                if i:
                    halve(i - 1)
                tile(i)
            halve(3)
            F_AT = 6
            P_AT, S_AT, ST_AT, V_AT, T_AT, W_AT, W3_AT, B_AT = (0, 1, 3, 4), (3, 6), 7, (8, 9, 11, 13), (5, 8, 10, 12), (7, 12, 14), 4, 6
            for u in range(-2, NU + 1):
                now, nxt, far, back = 0 <= u < NU, 0 <= u + 1 < NU, 0 <= u + 2 < NU, 0 <= u - 1 < NU
                new = u + 3 if u % 4 == 1 and u + 3 < NT else None
                val = u + 2 if u % 4 == 2 and u > 0 else u + 3 if u % 4 == 3 and u > 0 else None
                if val and val >= NT:
                    val = None
                b4 = u - 4 if u >= 4 and u % 4 == 0 else None
                sc = 0
                if u == NU - 1:
                    f2["load_router"](t_ST[u - 1])
                    f2["load_shared"](t_ST[u - 1])
                    f2["roots"](0, 12)
                if u == NU:
                    f2["logits"](11)
                for j in range(16):
                    if u == NU - 1 and 2 <= j < 14:
                        f2["tile"](j - 2, "dve", t_ST[u - 1], t_Vmm[NT - 1], t_P[NU - 1])
                        if j > 2:
                            f2["logits"](j - 3)
                    if now and j >= 3:
                        expo(u, j - 3)
                    if back and j < 3:
                        expo(u - 1, j + 13)
                    if nxt:
                        while sc < 16 and sc * 13 <= 16 * j:
                            scores(u + 1, sc)
                            sc += 1
                    if j == F_AT and 2 <= u + 3 < NU:
                        t_w[u + 3] = fetch(u + 3, t_P[u + 1])
                    if far and j in P_AT:
                        project(u + 2, P_AT.index(j) // 2, P_AT.index(j) % 2)
                    if far and j in S_AT:
                        split(u + 2, S_AT.index(j))
                    if far and j == ST_AT:
                        stack(u + 2)
                    if u == -2 and j in (8, 9, 10, 11):
                        value(j - 8, 0)
                        value(j - 8, 1)
                    if back and j == 1:
                        spread(u - 1)
                    if back and j == W3_AT:
                        weigh(u - 1, 3)
                        drain(u - 1)
                    if back and j == B_AT:
                        broadcast(u - 1)
                    if j == 3:
                        for i in {5: (0, 1), 6: (2, 3), 9: (4, 5), 10: (6, 7), 13: (8, 9), 14: (10, 11)}.get(u, ()):
                            f2["moments"](i)
                    if u == NU and j == 4:
                        f2["shared_up"](0, (0, 1), t_exp[16 * NU - 1])
                    if now and j in W_AT:
                        weigh(u, W_AT.index(j))
                    if val and j in V_AT:
                        value(val + V_AT.index(j) // 2, V_AT.index(j) % 2)
                    if new and j + 1 in T_AT:
                        center(new + T_AT.index(j + 1))
                    if u == -2 and j == 9:
                        for i in range(4):
                            residual(i)
                        stats(4, NT)
                    if new and j in (12, 13, 14, 15):
                        residual(new + j - 12)
                    if new and j in T_AT:
                        tile(new + T_AT.index(j))
                    if new and j - 1 in T_AT:
                        halve(new + T_AT.index(j - 1))
                    if nxt and j == 13:
                        rows(u + 1)
                    if nxt and j == 14:
                        fill(u + 1)
                    if nxt and j == 15:
                        invert(u + 1)
                    if b4 is not None and j in (8, 10, 12, 14):
                        result(b4 + (j - 8) // 2)
                        if b4 == NT - 4:
                            f2["moments"](b4 + (j - 8) // 2)
            return t_O[B - 1]

        y_d = nc.dram_tensor("y_d", [T, D], F32, kind="Internal").ap()
        f1 = ffn(0, y_d, [46 + 10 * r for r in range(7)], 35, 36, 116, 156, t_x)
        f1["load_router"]()
        f1["load_shared"](t_x)
        wf = [at("wf", (66 + 12 * c) * KB, [128, 3 * D], F32R) for c in range(4)]
        wh = [at("wh", (72 + 12 * c) * KB, [128, 3 * D], F32R) for c in range(4)]
        s_wf = [sem(f"s_wf{c}") for c in range(4)]
        t_wf = {}

        def load_weights(c):
            t_wf[c] = dma("sp", f"wf{c}", s_wf[c], lambda e: e.dma_start(
                wf[c][:, :].bitcast(F32), W_in.rearrange("(p c) n -> p c n", c=4)[:, c, :]), t_x)

        t_wl = []

        def split_weights(c):
            f = wf[c][:, :]
            h = op("act", lambda e: e.copy(wh[c][:, :], f.bitcast(F32)), t_wf[c])
            t_wl.append(op("pool", lambda e: e.tensor_tensor(f, f.bitcast(F32), wh[c][:, :].bitcast(F32), ALU.subtract), h))

        def store_parts():
            for c in range(4):
                for a, src in enumerate((wh[c], wf[c])):
                    v = src[:, :].bitcast(F32)
                    for k in range(2):
                        dma("sp", "wd", s_wd, lambda e, a=a, k=k, v=v, c=c: e.dma_start(
                            wqk_d[:, :, a, c, k, :].rearrange("g p n -> p g n"),
                            v[:, D * k:D * k + D].rearrange("p (g n) -> p g n", g=4)), t_wl[c])
                    t = dma("sp", "wd", s_wd, lambda e, a=a, v=v, c=c: e.dma_start(wv_d[:, a, c, :], v[:, 2 * D:3 * D]))
            return t

        def prepare():
            f1["load_ring"](range(2, 7), store_parts())

        for g in range(4):
            for i in range(4 * g, 4 * g + 4):
                f1["moments"](i)
            f1["roots"](4 * g, 4 * g + 4)
            for i in range(4 * g - 4, 4 * g + 4 if g == 3 else 4 * g):
                if i >= 0:
                    f1["tile"](i, "dve")
                    if i:
                        f1["logits"](i - 1)
                    if i in (1, 3, 5, 7):
                        load_weights(i // 2)
                    if i in (8, 10, 12, 14):
                        split_weights(i // 2 - 4)
        f1["logits"](NT - 1)
        f1["shared_up"](0)
        f1["load_ring"](range(2), t_x)
        t_y = f1["rest"](prepare)
        phase()
        s_y = [sem(f"s_yx{g}") for g in range(4)]
        def again(g):
            return dma("sp", f"yx{g}", s_y[g], lambda e: e.dma_start(
                X[:, 4 * g:4 * g + 4, :], y_d[512 * g:512 * g + 512, :].rearrange("(i p) d -> p i d", p=128)), t_y)

        s_y0 = [sem(f"s_y0{i}") for i in range(4)]
        t_x = [dma("sp", f"y0{i}", s_y0[i], lambda e, i=i: e.dma_start(X[:, i, :], y_d[128 * i:128 * i + 128, :]), t_y) for i in range(4)]
        t_w = {0: fetch(0)}
        trp = dma("sp", "rp", s_rp, lambda e: e.dma_start(rp[:, :, :], rope))
        t_x += [again(1)] * 4
        t_w[1] = fetch(1)
        t_x += [again(2)] * 4
        t_x += [again(3)] * 4
        for k in range(2):
            twv = dma("sp", "aw", s_aw, lambda e, k=k: e.dma_start(wv[k][:, :, :].bitcast(F32), wv_d[:, k, :, :]))
        two = dma("sp", "wo", s_wo, lambda e: e.dma_start(wout[:, :, :], W_out.rearrange("(c p) n -> p c n", c=4)))
        t_x2 = {}
        f2 = ffn(1, o_rows, [46, 36, 107, 117, 127, 137, 147], 66, 56, 67, 157, t_x2)
        t_att = attention(t_x, twv, trp, two, t_w, f2, t_x2)
        f2["roots"](12, NT)
        f2["shared_up"](0, (2, 3))
        for i in range(12, NT):
            f2["tile"](i, "dve")
            if i > 12:
                f2["logits"](i - 1)
        f2["logits"](NT - 1)
        f2["load_ring"](range(7), t_att)
        t_y = f2["rest"]()
        q.wait("pool", t_y)

        block = ctx.enter_context(nc.Block())
        block.sync(lambda e: q.emit("sp", e))
        block.scalar(lambda e: q.emit("act", e))
        block.vector(lambda e: q.emit("dve", e))
        block.gpsimd(lambda e: q.emit("pool", e))
        block.tensor(lambda e: q.emit("pe", e))


_INS = ["L0_attn_X", "L0_attn_ln_w", "L0_attn_ln_b", "L0_attn_W_in", "L0_attn_W_out", "L0_ffn_gate_w", "L0_ffn_bias",
        "L0_ffn_w_gate", "L0_ffn_w_up", "L0_ffn_w_down", "L0_ffn_ws_gate", "L0_ffn_ws_up", "L0_ffn_ws_down"]


def kernel(**inputs):
    import concourse.bacc as bacc
    from concourse.bass_utils import run_bass_kernel_spmd

    nc = bacc.Bacc("TRN2", target_bir_lowering=False, num_devices=1)
    given = {n: np.ascontiguousarray(inputs[n]) for n in _INS}
    given["consts"], given["rope"] = shape_constants()
    arrays, args = {}, []
    for n, a in given.items():
        arrays["in_" + n] = a
        args.append(nc.dram_tensor("in_" + n, a.shape, mybir.dt.from_np(a.dtype), kind="ExternalInput").ap())
    args.append(nc.dram_tensor("out_0", (B, S, D), F32, kind="ExternalOutput").ap())
    macaron_kernel(nc, *args)
    r = run_bass_kernel_spmd(nc, [arrays], core_ids=[0])
    return r.results[0]["out_0"]
```
